# Optimizing a Trainium2 kernel written in Bass

```python
import numpy as np
import jax
import jax.numpy as jnp

def _softmax(x, axis=-1):
    return jax.nn.softmax(x, axis=axis)

def _gelu(x):
    return jax.nn.gelu(x, approximate=True)

def _silu(x):
    return jax.nn.silu(x)

def _sigmoid(x):
    return jax.nn.sigmoid(x)

def _layernorm(x, axis=-1, eps=1e-05):
    m = jnp.mean(x, axis=axis, keepdims=True)
    v = jnp.var(x, axis=axis, keepdims=True)
    return (x - m) / jnp.sqrt(v + eps)

def _scatter_add(tgt, idx, src, axis=0):
    return tgt.at[idx].add(src)

def _segment_sum(src, seg, n):
    return jax.ops.segment_sum(src, seg, n)
kernel_name = 'mk_xattn_ffn_d1_seqx_r8_f20e63'

def setup_inputs(seed: int=0):
    np.random.seed(seed)
    _w = jnp.asarray

    def _rec_inputs():
        import jax
        import jax.numpy as jnp
        _rk = jax.random.key(seed)
        x = -0.0002928 + 1 * jax.random.normal(jax.random.fold_in(_rk, 1), (16, 128, 256), jnp.float32)
        _lenS = 128 - jax.random.randint(jax.random.fold_in(_rk, 7), (16,), 0, max(1, 128 // 4) + 1, jnp.int32)
        _lenS2 = 128 - jax.random.randint(jax.random.fold_in(_rk, 8), (16,), 0, max(1, 128 // 4) + 1, jnp.int32)
        fside_S2_0 = -0.00337071 + 1.01897 * jax.random.normal(jax.random.fold_in(_rk, 11), (128,), jnp.float32)
        _ctx_2048P = jax.random.normal(jax.random.fold_in(_rk, 12), (16, 16, 256), jnp.float32)
        _ctx_2048c = jax.random.dirichlet(jax.random.fold_in(_rk, 512), 0.3 * jnp.ones((16,), jnp.float32), (16, 128))
        _ctx_2048t = jnp.einsum('bsk,bkd->bsd', _ctx_2048c, _ctx_2048P)
        _ctx_2048t = _ctx_2048t * jax.lax.rsqrt(jnp.mean(jnp.square(_ctx_2048t)) + 1e-12) * 0.953939
        ctx_2048 = 0.000675642 + 1.00031 * (_ctx_2048t + 0.3 * jax.random.normal(jax.random.fold_in(_rk, 612), (16, 128, 256), jnp.float32))
        return (x, fside_S2_0, ctx_2048)
    x, fside_S2_0, ctx_2048 = _rec_inputs()

    def _L0_xattn_setup():
        import jax, jax.numpy as jnp
        import numpy as np
        key = jax.random.key(seed)
        ks = jax.random.split(key, 5)
        B, D, L, NH = (2, 128, 256, 8)
        H = D // NH
        return {'v': jax.random.normal(ks[0], (B, D, L), jnp.float32), 'k': jax.random.normal(ks[1], (H, L), jnp.float32) * 0.1, 'bias': jax.random.normal(ks[2], (D,), jnp.float32), 'x1': jax.random.normal(ks[3], (B, D, L), jnp.float32), 'x2': jax.random.normal(ks[4], (B, D, L), jnp.float32), 'num_heads': NH}
    _L0_xattn_all = _L0_xattn_setup()
    _L0_xattn_in = {k: v for k, v in _L0_xattn_all.items() if k in ('k',)}
    del _L0_xattn_all

    def _L0_ffn_setup():
        import jax, jax.numpy as jnp
        import numpy as np
        E, TOPK, H, I = (8, 2, 256, 512)
        SOFTCAP = 30.0
        key = jax.random.key(seed)
        ks = jax.random.split(key, 5)
        s = 1.0 / np.sqrt(H)
        si = 1.0 / np.sqrt(I)
        return {'hidden_states': jax.random.normal(ks[0], (4, 256, H), jnp.float32), 'w_gate': jax.random.normal(ks[1], (H, E), jnp.float32) * s, 'w1': jax.random.normal(ks[2], (E, H, I), jnp.float32) * s, 'w3': jax.random.normal(ks[3], (E, H, I), jnp.float32) * s, 'w2': jax.random.normal(ks[4], (E, I, H), jnp.float32) * si}
    _L0_ffn_all = _L0_ffn_setup()
    _L0_ffn_in = {k: v for k, v in _L0_ffn_all.items() if k in ('w_gate', 'w1', 'w3', 'w2')}
    del _L0_ffn_all
    return {'x': x, 'fside_S2_0': fside_S2_0, 'ctx_2048': ctx_2048, 'L0_xattn_k': _L0_xattn_in['k'], 'L0_ffn_w_gate': _L0_ffn_in['w_gate'], 'L0_ffn_w1': _L0_ffn_in['w1'], 'L0_ffn_w3': _L0_ffn_in['w3'], 'L0_ffn_w2': _L0_ffn_in['w2']}

def reference(x, fside_S2_0, ctx_2048, L0_xattn_k, L0_ffn_w_gate, L0_ffn_w1, L0_ffn_w3, L0_ffn_w2):
    import jax
    import jax.numpy as jnp

    def _L0_xattn_ref(v, k, bias, x1, x2, num_heads):
        import jax, jax.numpy as jnp
        import numpy as np
        B, D, L = v.shape
        H = D // num_heads
        fft_size = 2 * L
        vr = v.reshape(B, H, num_heads, L)
        x1r = x1.reshape(B, H, num_heads, L)
        x2r = x2.reshape(B, H, num_heads, L)
        kv = vr[:, :, :, None, :] * x2r[:, :, None, :, :]
        k_f = jnp.fft.rfft(k.astype(jnp.float32), n=fft_size)
        y = jnp.fft.irfft(jnp.fft.rfft(kv, n=fft_size) * k_f[None, :, None, None, :], n=fft_size)[..., :L]
        skip = bias.astype(jnp.float32).reshape(H, num_heads)[None, :, :, None, None]
        y = y + kv * skip
        out = jnp.einsum('bhijl,bhil->bhjl', y, x1r)
        return out.reshape(B, D, L)

    def _L0_ffn_ref(hidden_states, w_gate, w1, w3, w2):
        import jax, jax.numpy as jnp
        import numpy as np
        E, TOPK, H, I = (8, 2, 256, 512)
        SOFTCAP = 30.0
        orig_shape = hidden_states.shape
        x = hidden_states.reshape(-1, H)
        logits = x @ w_gate
        logits = SOFTCAP * jnp.tanh(logits / SOFTCAP)
        probs = jax.nn.softmax(logits, axis=-1)
        _, idx = jax.lax.top_k(probs, TOPK)
        mask = jax.nn.one_hot(idx, E, dtype=probs.dtype).sum(-2)
        weights = probs * mask
        out = jnp.zeros_like(x)
        for e in range(E):
            h = jax.nn.silu(x @ w1[e]) * (x @ w3[e])
            out = out + h @ w2[e] * weights[:, e:e + 1]
        return out.reshape(orig_shape)
    x = x + _L0_xattn_ref(_layernorm(x, axis=-1), L0_xattn_k, fside_S2_0, ctx_2048, ctx_2048, 8)
    x = x + _L0_ffn_ref(_layernorm(x, axis=-1), L0_ffn_w_gate, L0_ffn_w1, L0_ffn_w3, L0_ffn_w2)
    return x

_drawn_inputs = setup_inputs


def setup_inputs(seed=0):
    import zlib

    import numpy as np

    out = dict(_drawn_inputs(seed))
    spreads = {}
    factors = {}
    for name, (base, spread) in spreads.items():
        noise = np.random.default_rng([zlib.crc32(name.encode()), seed]).standard_normal(out[name].shape)
        drawn = base * np.exp(spread * noise) if base else spread * noise
        out[name] = jnp.asarray(drawn.astype(out[name].dtype))
    for name, factor in factors.items():
        out[name] = (out[name] * factor).astype(out[name].dtype)
    return out
```

```python
from contextlib import ExitStack

import concourse.bass as bass
from concourse import mybir

P = 128
F32 = mybir.dt.float32
I32 = mybir.dt.int32
ALU = mybir.AluOpType
ACT = mybir.ActivationFunctionType
AX = mybir.AxisListType

LN_EPS = 1e-5
SOFTCAP = 30.0
TOPK = 2


def xattn_ffn_kernel(nc, x, fside, ctx, k, w_gate, w1, w3, w2, out):
    B, D, L = x.shape
    H = k.shape[0]
    NH = D // H
    E = w_gate.shape[1]
    INNER = w1.shape[2]
    LB = L // P
    KB = INNER // P
    TOKENS = B * D
    CAP = TOKENS + P
    TILES = (TOPK * TOKENS + E * (P - 1)) // P
    SPARE = TILES - TOPK * TOKENS // P
    ROW = L + 2
    W_COL, ID_COL = L, L + 1
    CH = 512 // P
    NC = NH // CH
    assert B * NH == P and LB == 2 and NC == 2 and KB * P == 512 and H % 2 == 0

    kpad = nc.dram_tensor("kpad", (H, P + L), F32, kind="Internal").ap()
    regions = nc.dram_tensor("regions", (E * CAP + SPARE * P, ROW), F32, kind="Internal").ap()
    out_rows = out.rearrange("b d l -> (b d) l")

    def head_rows(t, h):
        return bass.AP(tensor=t.tensor, offset=h * (NH * L), ap=[[D * L, B], [L, NH], [1, L]])

    def split_rows(t):
        return t

    with ExitStack() as es:
        def sb(name, shape, dt=F32):
            return es.enter_context(nc.sbuf_tensor(name, shape, dt))

        def sem(name):
            return es.enter_context(nc.semaphore(name))

        def sems(name, n=2):
            return [sem(f"{name}{i}") for i in range(n)]

        ident = sb("ident", [P, P])
        ones = sb("ones", [P, P])
        earlier = sb("earlier", [P, P])
        same_b = sb("same_b", [P, B, NH])
        skip_mat = sb("skip_mat", [P, 2, P])
        bias_rows = sb("bias_rows", [H, B, NH])
        bias_pp = sb("bias_pp", [P, H])
        kin = sb("kin", [H, P + L])
        lower_e = sb("lower_e", [P, E, E])
        region_i = sb("region_i", [P, E], I32)
        region = sb("region", [P, E])
        choice_i = sb("choice_i", [P, TOPK], I32)
        choice = sb("choice", [P, TOPK])
        pid_i = sb("pid_i", [P, 1], I32)
        pid_b = sb("pid_b", [P, 1], I32)
        pid_f = sb("pid_f", [P, 1])
        pid_bf = sb("pid_bf", [P, 1])
        head_i = sb("head_i", [P, H], I32)
        head_f = sb("head_f", [P, H])
        row0 = sb("row0", [P, 1])
        out_row = sb("out_row", [P, H])
        filler = sb("filler", [P, ROW])
        neg_half = sb("neg_half", [P, 1])
        wg = sb("wg", [P, LB, E])
        W1 = sb("W1", [P, E, LB, INNER])
        W3 = sb("W3", [P, E, LB, INNER])
        W2 = sb("W2", [P, E, KB, L])
        xr = sb("xr", [P, 2, L])
        cr = sb("cr", [P, 2, L])
        hank = sb("hank", [P, H, L])
        toep = sb("toep", [P, 2, L])
        flip = sb("flip", [P, P])
        st1 = sb("st1", [P, 2, 6])
        mv1 = sb("mv1", [P, 2, 2])
        ve1 = sb("ve1", [P, 2, 1])
        rstd1 = sb("rstd1", [P, 2, 1])
        xhat = sb("xhat", [P, 2, L])
        u = sb("u", [P, 2, L])
        vcT = sb("vcT", [P, 2, 2, LB, P])
        kv = sb("kv", [P, 2, LB, NH, B, NH])
        z = sb("z", [P, LB, NH, P])
        mixT = sb("mixT", [P, 2, LB, P])
        base = sb("base", [P, 2, L])
        skip = sb("skip", [P, L])
        xn = sb("xn", [P, 2, L])
        st2 = sb("st2", [P, 2, 6])
        mv2 = sb("mv2", [P, 2, 2])
        ve2 = sb("ve2", [P, 2, 1])
        rstd2 = sb("rstd2", [P, 2, 1])
        rows = sb("rows", [P, 2, TOPK, ROW])
        xT2 = sb("xT2", [P, 2, LB, P])
        th = sb("th", [P, 2, E])
        tmax = sb("tmax", [P, 1])
        nbias = sb("nbias", [P, 1])
        ex = sb("ex", [P, E])
        esum = sb("esum", [P, 1])
        rsum = sb("rsum", [P, 1])
        prob = sb("prob", [P, E])
        gt = sb("gt", [P, E, E])
        eq = sb("eq", [P, E, E])
        eql = sb("eql", [P, E, E])
        ahead = sb("ahead", [P, E, E])
        order = sb("order", [P, E])
        hot = sb("hot", [P, TOPK, E])
        hotp = sb("hotp", [P, TOPK, E])
        mask = sb("mask", [P, E])
        msum = sb("msum", [P, 2, E])
        pos = sb("pos", [P, E])
        hpos = sb("hpos", [P, TOPK, E])
        destf = sb("destf", [P, TOPK])
        dest = sb("dest", [P, 2, TOPK], I32)
        fill_at = sb("fill_at", [1, E], I32)
        nt_i = sb("nt_i", [1, E], I32)
        nt_s = sb("nt_s", [1, E], I32)
        nt = sb("nt", [1, E])
        one_row = sb("one_row", [1, E])
        upto = sb("upto", [1, E])
        tile_i = sb("tile_i", [1, TILES], I32)
        tile_f = sb("tile_f", [1, TILES])
        past = sb("past", [1, TILES, E])
        past_nt = sb("past_nt", [1, TILES, E])
        eid = sb("eid", [1, TILES])
        first = sb("first", [1, TILES])
        inside = sb("inside", [1, TILES])
        reg_at = sb("reg_at", [1, TILES])
        tile_row = sb("tile_row", [1, TILES], I32)
        tile_expert = sb("tile_expert", [1, TILES], I32)
        xin = sb("xin", [P, 2, ROW])
        xT = sb("xT", [P, 2, LB, P])
        act1 = sb("act1", [P, 2, INNER])
        gated = sb("gated", [P, 2, INNER])
        gT = sb("gT", [P, 2, KB, P])
        ys = [sb(f"ys{q}", [P, L]) for q in range(2)]
        idx = [sb(f"idx{q}", [P, 1], I32) for q in range(4)]
        wt = sb("wt", [P, 4, 1])

        bank = [es.enter_context(nc.psum_tensor(f"bank{i}", [P, 512], F32)) for i in range(8)]
        conv_bank = [[bank[2 * m + c] for c in range(NC)] for m in range(LB)]
        vc_bank = bank[4]
        mix_bank = bank[5]
        skip_bank = bank[6]
        gate_bank = bank[7]
        h1_bank, h3_bank = bank[0:2], bank[2:4]
        xT_bank, gT_bank = bank[4], bank[5]
        y_bank = bank[6:8]

        s_consts = sem("s_consts")
        s_setup = sem("s_setup")
        s_bias = sem("s_bias")
        s_bias_ps = sem("s_bias_ps")
        s_bias_pp = sem("s_bias_pp")
        s_kin = sem("s_kin")
        s_kzero = sem("s_kzero")
        s_kpad = sem("s_kpad")
        s_wg = sem("s_wg")
        s_w = sem("s_w")
        s_diag = sem("s_diag")
        s_toepps = sem("s_toepps")
        s_toep = sem("s_toep")
        s_x, s_c = sems("s_x"), sems("s_c")
        s_mv1, s_mv1a, s_rstd1, s_xhat = sem("s_mv1"), sem("s_mv1a"), sem("s_rstd1"), sem("s_xhat")
        s_st1 = sem("s_st1")
        s_st2 = sem("s_st2")
        s_u = sem("s_u")
        s_smat = sem("s_smat")
        s_vcps = sem("s_vcps")
        s_vcT = sem("s_vcT")
        s_kv = sem("s_kv")
        s_conv = sem("s_conv")
        s_z = sem("s_z")
        s_mixT = sem("s_mixT")
        s_mixps = sem("s_mixps")
        s_skps = sem("s_skps")
        s_skip, s_base = sem("s_skip"), sem("s_base")
        s_xn, s_mv2, s_rstd2, s_mv2a = sem("s_xn"), sem("s_mv2"), sem("s_rstd2"), sem("s_mv2a")
        s_xst = sems("s_xst")
        s_rowA, s_rowB = sem("s_rowA"), sem("s_rowB")
        s_xT2ps, s_xT2 = sem("s_xT2ps"), sem("s_xT2")
        s_logit, s_th = sem("s_logit"), sem("s_th")
        s_tmax, s_nb, s_ex = sem("s_tmax"), sem("s_nb"), sem("s_ex")
        s_rsum, s_prob = sem("s_rsum"), sem("s_prob")
        s_gt, s_eq, s_eql, s_ahead = sem("s_gt"), sem("s_eq"), sem("s_eql"), sem("s_ahead")
        s_order, s_hot, s_hotp, s_mask = sem("s_order"), sem("s_hot"), sem("s_hotp"), sem("s_mask")
        s_wt, s_msum, s_rankps = sem("s_wt"), sem("s_msum"), sem("s_rankps")
        s_pos, s_hpos, s_destf, s_dest = sem("s_pos"), sem("s_hpos"), sem("s_destf"), sem("s_dest")
        s_id = sem("s_id")
        s_scat = sems("s_scat")
        s_fillw = sem("s_fillw")
        s_cnt = sem("s_cnt")
        s_tab = sem("s_tab")
        s_fill = sem("s_fill")
        s_xin = sems("s_xin")
        s_xTps, s_xT = sem("s_xTps"), sem("s_xT")
        s_h1, s_h3 = sem("s_h1"), sem("s_h3")
        s_act, s_gated = sem("s_act"), sem("s_gated")
        s_gTps, s_gT = sem("s_gTps"), sem("s_gT")
        s_y, s_ys, s_meta = sem("s_y"), sem("s_ys"), sem("s_meta")
        s_add = sems("s_add")

        s_apart = {nc.vector.engine: sem("s_apart_vector"), nc.gpsimd.engine: sem("s_apart_pool")}

        TABLE_STEPS = 14

        def after(eng, s, n):
            if not (isinstance(n, int) and n <= 0):
                eng.wait_ge(s, n)

        def wait_apart(eng, *waits):
            for s, n in waits:
                eng.wait_ge(s, n)
            eng.sem_inc(s_apart[eng.engine], 1)

        def loads(eng, pair, n, q):
            after(eng, pair[q], (n - q) * 8 + 16)

        def steps(eng, step, lags, count, unroll=2):
            top = max(lags)
            lo = -(-max(top, 2) // unroll) * unroll
            hi = lo + (count - lo) // unroll * unroll

            def live(t):
                return [0 <= t - g < count for g in lags]

            for t in range(lo):
                step(t, t % unroll, live(t))
            with eng.Fori(lo // unroll, hi // unroll) as i:
                for r in range(unroll):
                    step(i * unroll + r, r, [True] * len(lags))
            for t in range(hi, count + top):
                step(t, t % unroll, live(t))

        MIX_LAGS = [0, 1, 2, 3]

        block = es.enter_context(nc.Block())

        @block.sync
        def _(sp):
            sp.wait_ge(s_kzero, 1)
            sp.dma_start(kin[:, P:], k).then_inc(s_kin, 16)
            sp.dma_start(bias_rows[:, :, :], bass.AP(tensor=fside.tensor, offset=0,
                                                     ap=[[NH, H], [0, B], [1, NH]])).then_inc(s_bias, 16)
            sp.dma_start(wg[:, :, :], w_gate.rearrange("(c p) e -> p c e", p=P)).then_inc(s_wg, 16)
            sp.wait_ge(s_kin, 16)
            sp.dma_start(kpad, kin[:, :]).then_inc(s_kpad, 16)
            sp.wait_ge(s_kpad, 16)
            sp.dma_start(hank[:, :, :], bass.AP(tensor=kpad.tensor, offset=1,
                                                ap=[[1, P], [P + L, H], [1, L]])).then_inc(s_diag, 16)

            def step(t, q, live):
                prepare, _, to_rows, _ = live
                if prepare:
                    h = t
                    after(sp, s_base, h - 1)
                    after(sp, s_vcps, h - 1)
                    sp.dma_start(split_rows(xr[:, q, :]), head_rows(x, h)).then_inc(s_x[q], 16)
                    sp.dma_start(split_rows(cr[:, q, :]), head_rows(ctx, h)).then_inc(s_c[q], 16)
                if to_rows:
                    h = t - 2
                    sp.wait_ge(s_xn, h + 1)
                    sp.dma_start(head_rows(out, h), split_rows(xn[:, q, :])).then_inc(s_xst[q], 16)

            steps(sp, step, MIX_LAGS, H)

            sp.wait_ge(s_tab, 1)
            for e in range(E):
                at = sp.value_load(fill_at[0:1, e:e + 1], min_val=e * CAP, max_val=e * CAP + TOKENS)
                sp.dma_start(regions[bass.ds(at, P), :], filler[:, :]).then_inc(s_fill, 16)
            sp.wait_ge(s_tab, TABLE_STEPS)
            for q in range(2):
                sp.wait_ge(s_scat[q], H // 2 * TOPK * 16)
            sp.wait_ge(s_fill, E * 16)
            sp.wait_ge(s_fillw, SPARE * 16)

            def tile(s, q, live):
                at = sp.value_load(tile_row[0:1, bass.ds(s, 1)], min_val=0, max_val=E * CAP + (SPARE - 1) * P)
                after(sp, s_meta, s - 1)
                after(sp, s_xTps, s - 1)
                sp.dma_start(xin[:, q, :], regions[bass.ds(at, P), :]).then_inc(s_xin[q], 16)

            steps(sp, tile, [0], TILES)
            for q in range(2):
                sp.wait_ge(s_add[q], (TILES + 1 - q) // 2 * 16)

        @block.gpsimd
        def _(pool):
            pool.memset(ones[:, :], 1.0)
            pool.memset(ident[:, :], 0.0)
            pool.memset(flip[:, :], 0.0)
            pool.memset(earlier[:, :], 1.0)
            pool.memset(same_b[:, :, :], 1.0)
            pool.memset(lower_e[:, :, :], 1.0)
            pool.memset(filler[:, 0:ID_COL], 0.0)
            pool.memset(filler[:, ID_COL:ROW], float(TOKENS))
            pool.memset(neg_half[:, :], -0.5)
            pool.memset(msum[:, :, :], 0.0)
            pool.memset(one_row[:, :], 1.0)
            pool.iota(region_i[:, :], [[CAP, E]], base=0, channel_multiplier=0)
            pool.iota(choice_i[:, :], [[1, TOPK]], base=0, channel_multiplier=0)
            pool.iota(head_i[:, :], [[NH, H]], base=0, channel_multiplier=0)
            pool.iota(tile_i[:, :], [[1, TILES]], base=0, channel_multiplier=0)
            pool.iota(pid_i[:, :], [[0, 1]], base=0, channel_multiplier=1).then_inc(s_consts, 1)
            pool.wait_ge(s_consts, 1)
            pool.affine_select(out=ident[:, :], in_=ident[:, :], compare_op=ALU.not_equal, fill=1.0,
                               base=0, pattern=[[-1, P]], channel_multiplier=1)
            pool.affine_select(out=flip[:, :], in_=flip[:, :], compare_op=ALU.not_equal, fill=1.0,
                               base=1 - P, pattern=[[1, P]], channel_multiplier=1)
            pool.affine_select(out=earlier[:, :], in_=earlier[:, :], compare_op=ALU.is_ge, fill=0.0,
                               base=-1, pattern=[[1, P]], channel_multiplier=-1)
            pool.affine_select(out=lower_e[:, :, :], in_=lower_e[:, :, :], compare_op=ALU.is_ge, fill=0.0,
                               base=-1, pattern=[[1, E], [-1, E]], channel_multiplier=0)
            pool.affine_select(out=same_b[:, :, :], in_=same_b[:, :, :], compare_op=ALU.is_ge, fill=0.0,
                               base=0, pattern=[[-NH, B], [0, NH]], channel_multiplier=1).then_inc(s_consts, 1)
            pool.wait_ge(s_consts, 2)
            pool.affine_select(out=same_b[:, :, :], in_=same_b[:, :, :], compare_op=ALU.is_ge, fill=0.0,
                               base=NH - 1, pattern=[[NH, B], [0, NH]], channel_multiplier=-1).then_inc(s_consts, 1)

            for n in range(SPARE):
                pool.dma_start(regions[E * CAP + n * P:E * CAP + (n + 1) * P, :], filler[:, :]).then_inc(s_fillw, 16)

            def step(t, q, live):
                prepare, _, to_rows, route = live
                if prepare:
                    h = t
                    pool.wait_ge(s_mv1a, h + 1)
                    pool.tensor_tensor(rstd1[:, q, :], ve1[:, q, :], neg_half[:, :], ALU.pow).then_inc(s_rstd1, 1)
                if to_rows:
                    h = t - 2
                    pool.wait_ge(s_mv2a, h + 1)
                    pool.tensor_tensor(rstd2[:, q, :], ve2[:, q, :], neg_half[:, :], ALU.pow).then_inc(s_rstd2, 1)
                if prepare:
                    h = t
                    pool.wait_ge(s_xhat, h + 1)
                    loads(pool, s_c, h, q)
                    after(pool, s_skps, h - 1)
                    pool.tensor_tensor(u[:, q, :], xhat[:, q, :], cr[:, q, :], ALU.mult).then_inc(s_u, 1)
                    pool.wait_ge(s_vcT, h + 1)
                    after(pool, s_conv, (h - 1) * LB * NC)
                    for m in range(LB):
                        v = vcT[:, q, 0, m, :].rearrange("p (b i) -> p i b", i=NH)
                        c = vcT[:, q, 1, m, :].rearrange("p (b j) -> p b j", j=NH)
                        pool.tensor_tensor(kv[:, q, m],
                                           v.unsqueeze(3).to_broadcast([P, NH, B, NH]),
                                           c.unsqueeze(1).to_broadcast([P, NH, B, NH]),
                                           ALU.mult).then_inc(s_kv, 1)
                if route:
                    h = t - 3
                    r = 1 - q
                    if not (isinstance(h, int) and h < 2):
                        loads2 = (h - r - 2) * 16 + 32
                        pool.wait_ge(s_scat[r], loads2)
                    pool.tensor_copy(rows[:, r, :, ID_COL],
                                     out_row[:, bass.ds(h, 1)].to_broadcast([P, TOPK])).then_inc(s_id, 1)
                    wait_apart(pool, (s_id, h + 1), (s_dest, h + 1), (s_wt, h + 1), (s_rowB, h + 1))
                    for c in range(TOPK):
                        pool.indirect_dma_start(
                            out=regions, out_offset=bass.IndirectOffsetOnAxis(ap=dest[:, r, c:c + 1], axis=0),
                            in_=rows[:, r, c, :], in_offset=None).then_inc(s_scat[r], 16)

            pool.wait_ge(s_setup, 9)
            steps(pool, step, MIX_LAGS, H)
            for q in range(2):
                pool.wait_ge(s_xst[q], H // 2 * 16)

            def tile(s, q4, live):
                q = q4 % 2
                added = [] if isinstance(s, int) and s == 0 else [(s_add[1 - q], (s - 1 - (1 - q)) * 8 + 16)]
                wait_apart(pool, (s_ys, s + 1), (s_meta, s + 1), *added)
                pool.indirect_dma_start(
                    out=out_rows, out_offset=bass.IndirectOffsetOnAxis(ap=idx[q4][:, :], axis=0),
                    in_=ys[q][:, :], in_offset=None, bounds_check=TOKENS - 1, oob_is_err=False,
                    compute_op=ALU.add).then_inc(s_add[q], 16)

            steps(pool, tile, [0], TILES, 4)

        @block.scalar
        def _(act):
            act.wait_ge(s_bias_ps, 1)
            act.activation(bias_pp[:, :], mix_bank[:, 0:H], ACT.Copy).then_inc(s_bias_pp, 1)
            act.wait_ge(s_bias_pp, 1)
            act.wait_ge(s_consts, 3)

            def load_weights(e, part):
                if part == 0:
                    act.dma_start(W1[:, bass.ds(e, 1)].rearrange("p e c n -> p (e c) n"), bass.AP(
                        tensor=w1.tensor, offset=e * (L * INNER),
                        ap=[[INNER, P], [P * INNER, LB], [1, INNER]])).then_inc(s_w, 16)
                else:
                    act.dma_start(W3[:, bass.ds(e, 1)].rearrange("p e c n -> p (e c) n"), bass.AP(
                        tensor=w3.tensor, offset=e * (L * INNER),
                        ap=[[INNER, P], [P * INNER, LB], [1, INNER]])).then_inc(s_w, 16)
                    act.dma_start(W2[:, bass.ds(e, 1)].rearrange("p e c n -> p (e c) n"), bass.AP(
                        tensor=w2.tensor, offset=e * (L * INNER),
                        ap=[[L, P], [P * L, KB], [1, L]])).then_inc(s_w, 16)

            def step(t, q, live):
                prepare, _, to_rows, route = live
                r = 1 - q
                if route:
                    h = t - 3
                    act.wait_ge(s_logit, h + 1)
                    act.activation(th[:, r, :], gate_bank[:, L:L + E], ACT.Tanh, scale=1.0 / SOFTCAP).then_inc(s_th, 1)
                if prepare:
                    h = t
                    load_weights((t - q) // 2, q)
                    after(act, s_skps, h - 1)
                    act.activation(skip_mat[:, q, :], same_b[:, :, :].rearrange("p b j -> p (b j)"), ACT.Copy,
                                   scale=bias_pp[:, bass.ds(h, 1)]).then_inc(s_smat, 1)
                    act.wait_ge(s_vcps, h + 1)
                    after(act, s_z, (h - 1) * LB * NC)
                    after(act, s_kv, (h - 1) * LB)
                    act.activation(vcT[:, q].rearrange("p a m t -> p (a m t)"), vc_bank[:, :], ACT.Copy).then_inc(s_vcT, 1)
                if to_rows:
                    h = t - 2
                    act.wait_ge(s_rowA, h + 1)
                    act.activation(rows[:, q, 1, 0:L], rows[:, q, 0, 0:L], ACT.Copy).then_inc(s_rowB, 1)
                if prepare:
                    h = t
                    act.wait_ge(s_toepps, h + 1)
                    after(act, s_conv, (h - 1) * LB * NC)
                    act.activation(toep[:, q, :], vc_bank[:, 0:L], ACT.Copy).then_inc(s_toep, 1)
                if route:
                    h = t - 3
                    act.wait_ge(s_nb, h + 1)
                    act.activation(ex[:, :], th[:, r, :], ACT.Exp, bias=nbias[:, :], scale=SOFTCAP,
                                   accum_out=esum[:, :]).then_inc(s_ex, 1)
                if to_rows:
                    h = t - 2
                    act.wait_ge(s_xT2ps, h + 1)
                    after(act, s_logit, h - 1)
                    act.activation(xT2[:, q].rearrange("p m t -> p (m t)"), gate_bank[:, 0:L], ACT.Copy).then_inc(s_xT2, 1)

            steps(act, step, MIX_LAGS, H)

            def tile(s, q4, live):
                q = q4 % 2
                now_x, now_h, now_y = live
                if now_x:
                    act.wait_ge(s_xTps, s + 1)
                    after(act, s_h3, s - 1)
                    act.activation(xT[:, q].rearrange("p m t -> p (m t)"), xT_bank[:, 0:L], ACT.Copy).then_inc(s_xT, 1)
                if now_h:
                    n, r = s - 1, 1 - q
                    act.wait_ge(s_h1, n + 1)
                    after(act, s_gated, n - 1)
                    act.activation(act1[:, r, :], h1_bank[r][:, :], ACT.Silu).then_inc(s_act, 1)
                if now_y:
                    n = s - 2
                    act.wait_ge(s_y, n + 1)
                    act.wait_ge(s_meta, n + 1)
                    if not (isinstance(n, int) and n < 2):
                        loads(act, s_add, n - 2, q)
                    act.activation(ys[q][:, :], y_bank[q][:, 0:L], ACT.Copy,
                                   scale=wt[:, (q4 - 2) % 4, :]).then_inc(s_ys, 1)

            steps(act, tile, [0, 1, 2], TILES, 4)

        @block.vector
        def _(dve):
            dve.memset(kin[:, 0:P], 0.0).then_inc(s_kzero, 1)
            dve.wait_ge(s_consts, 3)
            dve.tensor_copy(region[:, :], region_i[:, :]).then_inc(s_setup, 1)
            dve.tensor_copy(choice[:, :], choice_i[:, :]).then_inc(s_setup, 1)
            dve.tensor_copy(head_f[:, :], head_i[:, :]).then_inc(s_setup, 1)
            dve.tensor_copy(tile_f[:, :], tile_i[:, :]).then_inc(s_setup, 1)
            dve.tensor_copy(pid_f[:, :], pid_i[:, :]).then_inc(s_setup, 1)
            dve.tensor_scalar(pid_b[:, :], pid_i[:, :], NH.bit_length() - 1, None,
                              ALU.logical_shift_right).then_inc(s_setup, 1)
            dve.wait_ge(s_setup, 6)
            dve.tensor_copy(pid_bf[:, :], pid_b[:, :]).then_inc(s_setup, 1)
            dve.wait_ge(s_setup, 7)
            dve.scalar_tensor_tensor(row0[:, :], pid_bf[:, :], float(D - NH), pid_f[:, :], ALU.mult,
                                     ALU.add).then_inc(s_setup, 1)
            dve.wait_ge(s_setup, 8)
            dve.tensor_scalar(out_row[:, :], head_f[:, :], row0[:, :], None, ALU.add).then_inc(s_setup, 1)

            def z_bank(h, q, m, c):
                n = (m * NC + c)
                dve.wait_ge(s_conv, h * (LB * NC) + n + 1)
                cb = vcT[:, q, 1, m, :].rearrange("p (b i) -> p i b", i=NH)[:, c * CH:(c + 1) * CH, :]
                dve.tensor_tensor(z[:, m, c * CH:(c + 1) * CH, :].rearrange("p i (b j) -> p i b j", b=B),
                                  conv_bank[m][c][:, :].rearrange("p (i b j) -> p i b j", i=CH, b=B),
                                  cb.unsqueeze(3).to_broadcast([P, CH, B, NH]), ALU.mult).then_inc(s_z, 1)

            def sum_i(h, q, m):
                dve.wait_ge(s_z, h * (LB * NC) + (m + 1) * NC)
                after(dve, s_mixps, h - 1)
                dve.tensor_reduce(mixT[:, q, m, :], z[:, m, :, :].rearrange("p i t -> p t i"), AX.X,
                                  ALU.add).then_inc(s_mixT, 1)

            def step(t, q, live):
                prepare, convolve, to_rows, route = live
                r = 1 - q
                if prepare:
                    h = t
                    loads(dve, s_x, h, q)
                    dve.bn_stats(st1[:, q, :], xr[:, q, :]).then_inc(s_st1, 1)
                    wait_apart(dve, (s_st1, h + 1))
                    dve.bn_aggr(mv1[:, q, :], st1[:, q, :]).then_inc(s_mv1, 1)
                    dve.wait_ge(s_mv1, h + 1)
                    dve.tensor_scalar(ve1[:, q, :], mv1[:, q, 1:2], LN_EPS, None, ALU.add).then_inc(s_mv1a, 1)
                if to_rows:
                    h = t - 2
                    dve.wait_ge(s_mixps, h + 1)
                    dve.wait_ge(s_base, h + 1)
                    if not (isinstance(h, int) and h < 2):
                        loads(dve, s_xst, h - 2, q)
                    dve.tensor_tensor(xn[:, q, :], mix_bank[:, 0:L], base[:, q, :], ALU.add).then_inc(s_xn, 1)
                    dve.wait_ge(s_xn, h + 1)
                    dve.bn_stats(st2[:, q, :], xn[:, q, :]).then_inc(s_st2, 1)
                    wait_apart(dve, (s_st2, h + 1))
                    dve.bn_aggr(mv2[:, q, :], st2[:, q, :]).then_inc(s_mv2, 1)
                    dve.wait_ge(s_mv2, h + 1)
                    dve.tensor_scalar(ve2[:, q, :], mv2[:, q, 1:2], LN_EPS, None, ALU.add).then_inc(s_mv2a, 1)
                if prepare:
                    h = t
                    dve.wait_ge(s_rstd1, h + 1)
                    after(dve, s_vcps, h - 1)
                    after(dve, s_u, h - 1)
                    dve.tensor_scalar(xhat[:, q, :], xr[:, q, :], mv1[:, q, 0:1], rstd1[:, q, :],
                                      ALU.subtract, ALU.mult).then_inc(s_xhat, 1)
                if convolve:
                    z_bank(t - 1, r, 0, 0)
                    z_bank(t - 1, r, 0, 1)
                if to_rows:
                    h = t - 2
                    dve.wait_ge(s_rstd2, h + 1)
                    if not (isinstance(h, int) and h < 2):
                        dve.wait_ge(s_scat[q], (h - q - 2) * 16 + 32)
                    dve.tensor_scalar(rows[:, q, 0, 0:L], xn[:, q, :], mv2[:, q, 0:1], rstd2[:, q, :],
                                      ALU.subtract, ALU.mult).then_inc(s_rowA, 1)
                if route:
                    h = t - 3
                    dve.wait_ge(s_th, h + 1)
                    dve.tensor_reduce(tmax[:, :], th[:, r, :], AX.X, ALU.max).then_inc(s_tmax, 1)
                    dve.wait_ge(s_tmax, h + 1)
                    dve.tensor_scalar(nbias[:, :], tmax[:, :], -SOFTCAP, None, ALU.mult).then_inc(s_nb, 1)
                if convolve:
                    sum_i(t - 1, r, 0)
                    z_bank(t - 1, r, 1, 0)
                    z_bank(t - 1, r, 1, 1)
                if route:
                    h = t - 3
                    dve.wait_ge(s_ex, h + 1)
                    dve.reciprocal(rsum[:, :], esum[:, :]).then_inc(s_rsum, 1)
                    dve.wait_ge(s_rsum, h + 1)
                    dve.tensor_scalar(prob[:, :], ex[:, :], rsum[:, :], None, ALU.mult).then_inc(s_prob, 1)
                    dve.wait_ge(s_prob, h + 1)
                    pf = prob[:, :].unsqueeze(1).to_broadcast([P, E, E])
                    pe = prob[:, :].unsqueeze(2).to_broadcast([P, E, E])
                    dve.tensor_tensor(eq[:, :, :], pf, pe, ALU.is_equal).then_inc(s_eq, 1)
                    dve.tensor_tensor(gt[:, :, :], pf, pe, ALU.is_gt).then_inc(s_gt, 1)
                    dve.wait_ge(s_eq, h + 1)
                    dve.tensor_tensor(eql[:, :, :], eq[:, :, :], lower_e[:, :, :], ALU.mult).then_inc(s_eql, 1)
                    dve.wait_ge(s_eql, h + 1)
                    dve.wait_ge(s_gt, h + 1)
                    dve.tensor_tensor(ahead[:, :, :], gt[:, :, :], eql[:, :, :], ALU.add).then_inc(s_ahead, 1)
                    dve.wait_ge(s_ahead, h + 1)
                    dve.tensor_reduce(order[:, :], ahead[:, :, :], AX.X, ALU.add).then_inc(s_order, 1)
                    dve.wait_ge(s_order, h + 1)
                    after(dve, s_rankps, h)
                    dve.tensor_scalar(mask[:, :], order[:, :], float(TOPK), None, ALU.is_lt).then_inc(s_mask, 1)
                if prepare:
                    h = t
                    loads(dve, s_c, h, q)
                    dve.wait_ge(s_skps, h + 1)
                    dve.tensor_tensor(skip[:, :], skip_bank[:, 0:L], cr[:, q, :], ALU.mult).then_inc(s_skip, 1)
                    dve.wait_ge(s_skip, h + 1)
                    dve.tensor_tensor(base[:, q, :], skip[:, :], xr[:, q, :], ALU.add).then_inc(s_base, 1)
                if convolve:
                    sum_i(t - 1, r, 1)
                if route:
                    h = t - 3
                    dve.tensor_tensor(hot[:, :, :], order[:, :].unsqueeze(1).to_broadcast([P, TOPK, E]),
                                      choice[:, :].unsqueeze(2).to_broadcast([P, TOPK, E]),
                                      ALU.is_equal).then_inc(s_hot, 1)
                    dve.wait_ge(s_mask, h + 1)
                    dve.tensor_tensor(msum[:, 1 - r, :], msum[:, r, :], mask[:, :], ALU.add).then_inc(s_msum, 1)
                    dve.wait_ge(s_hot, h + 1)
                    dve.tensor_tensor(hotp[:, :, :], hot[:, :, :],
                                      prob[:, :].unsqueeze(1).to_broadcast([P, TOPK, E]), ALU.mult).then_inc(s_hotp, 1)
                    dve.wait_ge(s_rankps, h + 1)
                    dve.tensor_tensor(pos[:, :], skip_bank[:, L:L + E], region[:, :], ALU.add).then_inc(s_pos, 1)
                    dve.wait_ge(s_hotp, h + 1)
                    dve.tensor_reduce(rows[:, r, :, W_COL], hotp[:, :, :], AX.X, ALU.add).then_inc(s_wt, 1)
                    dve.wait_ge(s_pos, h + 1)
                    dve.tensor_tensor(hpos[:, :, :], hot[:, :, :],
                                      pos[:, :].unsqueeze(1).to_broadcast([P, TOPK, E]), ALU.mult).then_inc(s_hpos, 1)
                    dve.wait_ge(s_hpos, h + 1)
                    dve.tensor_reduce(destf[:, :], hpos[:, :, :], AX.X, ALU.add).then_inc(s_destf, 1)
                    dve.wait_ge(s_destf, h + 1)
                    dve.tensor_copy(dest[:, r, :], destf[:, :]).then_inc(s_dest, 1)

            steps(dve, step, MIX_LAGS, H)

            chain = [0]

            def link(ins):
                ins.then_inc(s_tab, 1)
                chain[0] += 1
                dve.wait_ge(s_tab, chain[0])

            dve.wait_ge(s_cnt, 1)
            cnt = skip_bank[0:1, 0:E]
            link(dve.tensor_tensor(fill_at[:, :], cnt, region[0:1, :], ALU.add))
            link(dve.tensor_scalar(nt_i[:, :], cnt, float(P - 1), None, ALU.add))
            link(dve.tensor_scalar(nt_s[:, :], nt_i[:, :], P.bit_length() - 1, None, ALU.logical_shift_right))
            link(dve.tensor_copy(nt[:, :], nt_s[:, :]))
            link(dve.tensor_tensor_scan(upto[:, :], one_row[:, :], nt[:, :], 0.0, ALU.mult, ALU.add))
            link(dve.tensor_tensor(past[:, :, :], tile_f[:, :].unsqueeze(2).to_broadcast([1, TILES, E]),
                                   upto[:, :].unsqueeze(1).to_broadcast([1, TILES, E]), ALU.is_ge))
            link(dve.tensor_tensor(past_nt[:, :, :], past[:, :, :],
                                   nt[:, :].unsqueeze(1).to_broadcast([1, TILES, E]), ALU.mult))
            link(dve.tensor_reduce(eid[:, :], past[:, :, :], AX.X, ALU.add))
            link(dve.tensor_reduce(first[:, :], past_nt[:, :, :], AX.X, ALU.add))
            link(dve.tensor_scalar(tile_expert[:, :], eid[:, :], float(E - 1), None, ALU.min))
            link(dve.tensor_tensor(inside[:, :], tile_f[:, :], first[:, :], ALU.subtract))
            link(dve.tensor_scalar(reg_at[:, :], eid[:, :], float(CAP), None, ALU.mult))
            link(dve.tensor_scalar(first[:, :], inside[:, :], float(P), None, ALU.mult))
            link(dve.tensor_tensor(tile_row[:, :], first[:, :], reg_at[:, :], ALU.add))
            assert chain[0] == TABLE_STEPS

            def tile(s, q4, live):
                q = q4 % 2
                now_meta, now_h, now_y = live
                if now_y:
                    n = s - 2
                    dve.wait_ge(s_gTps, n + 1)
                    after(dve, s_y, n - 1)
                    dve.tensor_copy(gT[:, q].rearrange("p m t -> p (m t)"), gT_bank[:, :]).then_inc(s_gT, 1)
                if now_meta:
                    loads(dve, s_xin, s, q)
                    if not (isinstance(s, int) and s < 4):
                        loads(dve, s_add, s - 4, q)
                    dve.tensor_copy(wt[:, q4, :], xin[:, q, W_COL:W_COL + 1])
                    dve.tensor_copy(idx[q4][:, :], xin[:, q, ID_COL:ROW]).then_inc(s_meta, 1)
                if now_h:
                    n, r = s - 1, 1 - q
                    dve.wait_ge(s_act, n + 1)
                    dve.wait_ge(s_h3, n + 1)
                    after(dve, s_gTps, n - 1)
                    dve.tensor_tensor(gated[:, r, :], act1[:, r, :], h3_bank[r][:, :], ALU.mult).then_inc(s_gated, 1)

            steps(dve, tile, [0, 1, 2], TILES, 4)

        @block.tensor
        def _(pe):
            pe.wait_ge(s_consts, 3)
            pe.wait_ge(s_bias, 16)
            pe.transpose(mix_bank[:, 0:H], bias_rows[:, :, :].rearrange("h b i -> h (b i)"),
                         ident[0:H, 0:H]).then_inc(s_bias_ps, 1)
            pe.wait_ge(s_wg, 16)
            pe.wait_ge(s_bias_pp, 1)
            pe.wait_ge(s_diag, 16)

            def conv(h, q, m):
                for c in range(NC):
                    after(pe, s_z, (h - 1) * (LB * NC) + m * NC + c + 1)
                    for n in range(m + 1):
                        mm = pe.matmul(conv_bank[m][c][:, :],
                                       toep[:, q, (m - n) * P:(m - n + 1) * P],
                                       kv[:, q, n, c * CH:(c + 1) * CH].rearrange("p i b j -> p (i b j)"),
                                       start=(n == 0), stop=(n == m))
                    mm.then_inc(s_conv, 1)

            def step(t, q, live):
                prepare, convolve, to_rows, route = live
                r = 1 - q
                if route:
                    h = t - 3
                    pe.wait_ge(s_xT2, h + 1)
                    for m in range(LB):
                        mm = pe.matmul(gate_bank[:, L:L + E], xT2[:, r, m, :], wg[:, m, :],
                                       start=(m == 0), stop=(m == LB - 1))
                    mm.then_inc(s_logit, 1)
                if to_rows:
                    h = t - 2
                    pe.wait_ge(s_mixT, (h + 1) * LB)
                    after(pe, s_xn, h)
                    for m in range(LB):
                        mm = pe.transpose(mix_bank[:, m * P:(m + 1) * P], mixT[:, q, m, :], ident[:, :])
                    mm.then_inc(s_mixps, 1)
                if convolve:
                    h = t - 1
                    pe.wait_ge(s_kv, (h + 1) * LB)
                    pe.wait_ge(s_toep, h + 1)
                    conv(h, r, 0)
                if prepare:
                    h = t
                    pe.wait_ge(s_xhat, h + 1)
                    loads(pe, s_c, h, q)
                    after(pe, s_toep, h)
                    for a, src in ((0, xhat), (1, cr)):
                        for m in range(LB):
                            mm = pe.transpose(vc_bank[:, (a * LB + m) * P:(a * LB + m + 1) * P],
                                              src[:, q, m * P:(m + 1) * P], ident[:, :])
                    mm.then_inc(s_vcps, 1)
                if convolve:
                    conv(t - 1, r, 1)
                if prepare:
                    h = t
                    pe.wait_ge(s_u, h + 1)
                    if not (isinstance(h, int) and h < 4):
                        pe.wait_ge(s_pos, h - 3)
                    after(pe, s_skip, h)
                    pe.wait_ge(s_smat, h + 1)
                    mm = pe.matmul(skip_bank[:, 0:L], skip_mat[:, q, :], u[:, q, :], start=True, stop=True)
                    mm.then_inc(s_skps, 1)
                    pe.wait_ge(s_vcT, h + 1)
                    pe.matmul(vc_bank[:, 0:L], flip[:, :], hank[:, bass.ds(h, 1), :].rearrange("p a l -> p (a l)"),
                              start=True, stop=True).then_inc(s_toepps, 1)
                if to_rows:
                    h = t - 2
                    pe.wait_ge(s_rowA, h + 1)
                    after(pe, s_th, h)
                    for m in range(LB):
                        mm = pe.transpose(gate_bank[:, m * P:(m + 1) * P], rows[:, q, 0, m * P:(m + 1) * P], ident[:, :])
                    mm.then_inc(s_xT2ps, 1)
                if route:
                    h = t - 3
                    pe.wait_ge(s_mask, h + 1)
                    after(pe, s_msum, h)
                    if prepare:
                        pe.wait_ge(s_skip, t + 1)
                    after(pe, s_pos, h)
                    pe.matmul(skip_bank[:, L:L + E], earlier[:, :], mask[:, :], start=True, stop=False)
                    pe.matmul(skip_bank[:, L:L + E], ones[:, :], msum[:, r, :], start=False, stop=True).then_inc(s_rankps, 1)

            steps(pe, step, MIX_LAGS, H)
            pe.wait_ge(s_msum, H)
            pe.wait_ge(s_pos, H)
            pe.matmul(skip_bank[:, 0:E], ones[:, :], msum[:, H % 2, :], start=True, stop=True).then_inc(s_cnt, 1)

            pe.wait_ge(s_w, 3 * E * 16)
            pe.wait_ge(s_tab, TABLE_STEPS)
            pe.wait_ge(s_z, H * LB * NC)

            def tile(s, q4, live):
                q = q4 % 2
                now_x, now_h, now_y = live
                if now_x:
                    loads(pe, s_xin, s, q)
                    after(pe, s_xT, s)
                    for m in range(LB):
                        mm = pe.transpose(xT_bank[:, m * P:(m + 1) * P], xin[:, q, m * P:(m + 1) * P], ident[:, :])
                    mm.then_inc(s_xTps, 1)
                if now_h:
                    n, r = s - 1, 1 - q
                    e = pe.value_load(tile_expert[0:1, bass.ds(n, 1)], min_val=0, max_val=E - 1)
                    pe.wait_ge(s_xT, n + 1)
                    after(pe, s_act, n - 1)
                    for m in range(LB):
                        mm = pe.matmul(h1_bank[r][:, :], xT[:, r, m, :],
                                       W1[:, bass.ds(e, 1), m, :], start=(m == 0), stop=(m == LB - 1))
                    mm.then_inc(s_h1, 1)
                if now_y:
                    n = s - 2
                    pe.wait_ge(s_gated, n + 1)
                    after(pe, s_gT, n)
                    for m in range(KB):
                        mm = pe.transpose(gT_bank[:, m * P:(m + 1) * P], gated[:, q, m * P:(m + 1) * P], ident[:, :])
                    mm.then_inc(s_gTps, 1)
                if now_h:
                    n, r = s - 1, 1 - q
                    after(pe, s_gated, n - 1)
                    for m in range(LB):
                        mm = pe.matmul(h3_bank[r][:, :], xT[:, r, m, :],
                                       W3[:, bass.ds(e, 1), m, :], start=(m == 0), stop=(m == LB - 1))
                    mm.then_inc(s_h3, 1)
                if now_y:
                    n = s - 2
                    e = pe.value_load(tile_expert[0:1, bass.ds(n, 1)], min_val=0, max_val=E - 1)
                    pe.wait_ge(s_gT, n + 1)
                    after(pe, s_ys, n - 1)
                    for m in range(KB):
                        mm = pe.matmul(y_bank[q][:, 0:L], gT[:, q, m, :],
                                       W2[:, bass.ds(e, 1), m, :], start=(m == 0), stop=(m == KB - 1))
                    mm.then_inc(s_y, 1)

            steps(pe, tile, [0, 1, 2], TILES, 4)


_INS = ['x', 'fside_S2_0', 'ctx_2048', 'L0_xattn_k', 'L0_ffn_w_gate', 'L0_ffn_w1', 'L0_ffn_w3', 'L0_ffn_w2']
_OUTS = [((16, 128, 256), 'float32')]


def kernel(**inputs):
    import numpy as _np
    import concourse.bacc as _bacc
    from concourse import mybir as _mybir
    from concourse.bass_utils import run_bass_kernel_spmd as _run

    nc = _bacc.Bacc("TRN2", target_bir_lowering=False, num_devices=1)
    arrays, args = {}, []
    for name in _INS:
        a = _np.ascontiguousarray(inputs[name])
        arrays[f"in_{name}_dram"] = a
        args.append(nc.dram_tensor(f"in_{name}_dram", a.shape, _mybir.dt.from_np(a.dtype), kind="ExternalInput").ap())
    for i, (shape, dtype) in enumerate(_OUTS):
        dt = _mybir.dt.from_np(_np.dtype(dtype))
        args.append(nc.dram_tensor(f"out_{i}_dram", shape, dt, kind="ExternalOutput").ap())
    xattn_ffn_kernel(nc, *args)
    r = _run(nc, [arrays], core_ids=[0])
    got = tuple(r.results[0][f"out_{i}_dram"] for i in range(len(_OUTS)))
    return got[0]
```

```python
from contextlib import ExitStack

import concourse.bass as bass
from concourse import mybir

P = 128
F32 = mybir.dt.float32
I32 = mybir.dt.int32
ALU = mybir.AluOpType
ACT = mybir.ActivationFunctionType
AX = mybir.AxisListType

LN_EPS = 1e-5
SOFTCAP = 30.0
TOPK = 2


def xattn_ffn_kernel(nc, x, fside, ctx, k, w_gate, w1, w3, w2, out):
    B, D, L = x.shape
    H = k.shape[0]
    NH = D // H
    E = w_gate.shape[1]
    INNER = w1.shape[2]
    LB = L // P
    KB = INNER // P
    TOKENS = B * D
    CAP = TOKENS + P
    TILES = (TOPK * TOKENS + E * (P - 1)) // P
    SPARE = TILES - TOPK * TOKENS // P
    ROW = L + 2
    W_COL, ID_COL = L, L + 1
    CH = 512 // P
    NC = NH // CH
    assert B * NH == P and LB == 2 and NC == 2 and KB * P == 512 and H % 2 == 0

    kpad = nc.dram_tensor("kpad", (H, P + L), F32, kind="Internal").ap()
    regions = nc.dram_tensor("regions", (E * CAP + SPARE * P, ROW), F32, kind="Internal").ap()
    out_rows = out.rearrange("b d l -> (b d) l")

    def head_rows(t, h):
        return bass.AP(tensor=t.tensor, offset=h * (NH * L), ap=[[D * L, B], [L, NH], [1, L]])

    def split_rows(t):
        return t

    with ExitStack() as es:
        def sb(name, shape, dt=F32):
            return es.enter_context(nc.sbuf_tensor(name, shape, dt))

        def sem(name):
            return es.enter_context(nc.semaphore(name))

        def sems(name, n=2):
            return [sem(f"{name}{i}") for i in range(n)]

        ident = sb("ident", [P, P])
        ones = sb("ones", [P, P])
        earlier = sb("earlier", [P, P])
        same_b = sb("same_b", [P, B, NH])
        skip_mat = sb("skip_mat", [P, 2, P])
        bias_rows = sb("bias_rows", [H, B, NH])
        bias_pp = sb("bias_pp", [P, H])
        kin = sb("kin", [H, P + L])
        lower_e = sb("lower_e", [P, E, E])
        region_i = sb("region_i", [P, E], I32)
        region = sb("region", [P, E])
        choice_i = sb("choice_i", [P, TOPK], I32)
        choice = sb("choice", [P, TOPK])
        pid_i = sb("pid_i", [P, 1], I32)
        pid_b = sb("pid_b", [P, 1], I32)
        pid_f = sb("pid_f", [P, 1])
        pid_bf = sb("pid_bf", [P, 1])
        head_i = sb("head_i", [P, H], I32)
        head_f = sb("head_f", [P, H])
        row0 = sb("row0", [P, 1])
        out_row = sb("out_row", [P, H])
        filler = sb("filler", [P, ROW])
        neg_half = sb("neg_half", [P, 1])
        wg = sb("wg", [P, LB, E])
        silu0 = sb("silu0", [P, 1])
        W1 = sb("W1", [P, E, LB, INNER])
        W3 = sb("W3", [P, E, LB, INNER])
        W2 = sb("W2", [P, E, KB, L])
        xr = sb("xr", [P, 4, L])
        cr = sb("cr", [P, 4, L])
        hank = sb("hank", [P, H, L])
        toep = sb("toep", [P, 2, L])
        flip = sb("flip", [P, P])
        sum1 = sb("sum1", [P, 2, 1])
        nm1 = sb("nm1", [P, 2, 1])
        ssq1 = sb("ssq1", [P, 2, 1])
        junk = sb("junk", [P, L])
        ve1 = sb("ve1", [P, 2, 1])
        nmr1 = sb("nmr1", [P, 2, 1])
        rstd1 = sb("rstd1", [P, 2, 1])
        xhat = sb("xhat", [P, 2, L])
        u = sb("u", [P, 2, L])
        vcT = sb("vcT", [P, 2, 2, LB, P])
        kv = sb("kv", [P, 2, LB, NH, B, NH])
        z = sb("z", [P, LB, NH, P])
        mixT = sb("mixT", [P, 2, LB, P])
        base = sb("base", [P, 2, L])
        skip = sb("skip", [P, L])
        xn = sb("xn", [P, 2, L])
        st2 = sb("st2", [P, 2, 6])
        mv2 = sb("mv2", [P, 2, 2])
        ve2 = sb("ve2", [P, 2, 1])
        nmr2 = sb("nmr2", [P, 2, 1])
        rstd2 = sb("rstd2", [P, 2, 1])
        rows = sb("rows", [P, 4, TOPK, ROW])
        xT2 = sb("xT2", [P, 2, LB, P])
        th = sb("th", [P, 2, E])
        tmax = sb("tmax", [P, 1])
        nbias = sb("nbias", [P, 1])
        ex = sb("ex", [P, E])
        esum = sb("esum", [P, 1])
        rsum = sb("rsum", [P, 1])
        prob = sb("prob", [P, E])
        gt = sb("gt", [P, E, E])
        eq = sb("eq", [P, E, E])
        eql = sb("eql", [P, E, E])
        ahead = sb("ahead", [P, E, E])
        order = sb("order", [P, E])
        hot = sb("hot", [P, TOPK, E])
        hotp = sb("hotp", [P, TOPK, E])
        mask = sb("mask", [P, E])
        msum = sb("msum", [P, 2, E])
        pos = sb("pos", [P, E])
        hpos = sb("hpos", [P, TOPK, E])
        destf = sb("destf", [P, TOPK])
        dest = sb("dest", [P, 4, TOPK], I32)
        fill_at = sb("fill_at", [1, E], I32)
        nt_i = sb("nt_i", [1, E], I32)
        nt_s = sb("nt_s", [1, E], I32)
        nt = sb("nt", [1, E])
        one_row = sb("one_row", [1, E])
        upto = sb("upto", [1, E])
        tile_i = sb("tile_i", [1, TILES], I32)
        tile_f = sb("tile_f", [1, TILES])
        past = sb("past", [1, TILES, E])
        past_nt = sb("past_nt", [1, TILES, E])
        eid = sb("eid", [1, TILES])
        first = sb("first", [1, TILES])
        inside = sb("inside", [1, TILES])
        reg_at = sb("reg_at", [1, TILES])
        tile_row = sb("tile_row", [1, TILES], I32)
        tile_expert = sb("tile_expert", [1, TILES], I32)
        xin = sb("xin", [P, 2, ROW])
        xT = sb("xT", [P, 2, LB, P])
        act1 = sb("act1", [P, 2, INNER])
        gated = sb("gated", [P, 2, INNER])
        gT = sb("gT", [P, 2, KB, P])
        ys = [sb(f"ys{q}", [P, L]) for q in range(2)]
        idx = [sb(f"idx{q}", [P, 1], I32) for q in range(4)]
        wt = sb("wt", [P, 4, 1])

        bank = [es.enter_context(nc.psum_tensor(f"bank{i}", [P, 512], F32)) for i in range(8)]
        conv_bank = [[bank[2 * m + c] for c in range(NC)] for m in range(LB)]
        vc_bank = bank[4]
        mix_bank = bank[5]
        skip_bank = bank[6]
        gate_bank = bank[7]
        h1_bank, h3_bank = bank[0:2], bank[2:4]
        xT_bank, gT_bank = bank[4], bank[5]
        y_bank = bank[6:8]

        s_consts = sem("s_consts")
        s_setup = sem("s_setup")
        s_bias = sem("s_bias")
        s_bias_ps = sem("s_bias_ps")
        s_bias_pp = sem("s_bias_pp")
        s_filler = sem("s_filler")
        s_kin = sem("s_kin")
        s_kzero = sem("s_kzero")
        s_kpad = sem("s_kpad")
        s_wg = sem("s_wg")
        s_w = sem("s_w")
        s_diag = sem("s_diag")
        s_toepps = sem("s_toepps")
        s_toep = sem("s_toep")
        s_x, s_c = sems("s_x", 4), sems("s_c", 4)
        s_sum1, s_nm1, s_ssq1, s_ve1 = sem("s_sum1"), sem("s_nm1"), sem("s_ssq1"), sem("s_ve1")
        s_rstd1, s_nmr1, s_xhat = sem("s_rstd1"), sem("s_nmr1"), sem("s_xhat")
        s_st2 = sem("s_st2")
        s_u = sem("s_u")
        s_smat = sem("s_smat")
        s_vcps = sem("s_vcps")
        s_vcT = sem("s_vcT")
        s_kv = sem("s_kv")
        s_conv = sem("s_conv")
        s_z = sem("s_z")
        s_mixT = sem("s_mixT")
        s_mixps = sem("s_mixps")
        s_skps = sem("s_skps")
        s_skip, s_base = sem("s_skip"), sem("s_base")
        s_xn, s_mv2, s_rstd2, s_mv2a = sem("s_xn"), sem("s_mv2"), sem("s_rstd2"), sem("s_mv2a")
        s_xst = sems("s_xst")
        s_rowA, s_rowB = sem("s_rowA"), sem("s_rowB")
        s_xT2ps, s_xT2 = sem("s_xT2ps"), sem("s_xT2")
        s_logit, s_th = sem("s_logit"), sem("s_th")
        s_tmax, s_nb, s_ex = sem("s_tmax"), sem("s_nb"), sem("s_ex")
        s_rsum, s_prob = sem("s_rsum"), sem("s_prob")
        s_gt, s_eq, s_eql, s_ahead = sem("s_gt"), sem("s_eq"), sem("s_eql"), sem("s_ahead")
        s_order, s_hot, s_hotp, s_mask = sem("s_order"), sem("s_hot"), sem("s_hotp"), sem("s_mask")
        s_wt, s_msum, s_rankps = sem("s_wt"), sem("s_msum"), sem("s_rankps")
        s_pos, s_hpos, s_destf, s_dest = sem("s_pos"), sem("s_hpos"), sem("s_destf"), sem("s_dest")
        s_id = sem("s_id")
        s_scat = sems("s_scat", 4)
        s_nmr2 = sem("s_nmr2")
        s_fillw = sem("s_fillw")
        s_cnt = sem("s_cnt")
        s_tab = sem("s_tab")
        s_fill = sems("s_fill", 3)
        s_xin = sems("s_xin")
        s_xTps, s_xT = sem("s_xTps"), sem("s_xT")
        s_h1, s_h3 = sem("s_h1"), sem("s_h3")
        s_act, s_gated = sem("s_act"), sem("s_gated")
        s_gTps, s_gT = sem("s_gTps"), sem("s_gT")
        s_y, s_ys, s_meta = sem("s_y"), sem("s_ys"), sem("s_meta")
        s_add = sems("s_add")

        s_apart = {nc.vector.engine: sem("s_apart_vector"), nc.gpsimd.engine: sem("s_apart_pool")}

        TABLE_STEPS = 14

        def after(eng, s, n):
            if not (isinstance(n, int) and n <= 0):
                eng.wait_ge(s, n)

        def wait_apart(eng, *waits):
            for s, n in waits:
                eng.wait_ge(s, n)
            eng.sem_inc(s_apart[eng.engine], 1)

        def loads(eng, pair, n, q):
            after(eng, pair[q], (n - q) * 8 + 16)

        def scattered(eng, h, h4):
            if not (isinstance(h, int) and h < 0):
                eng.wait_ge(s_scat[h4], (h - h4) * 8 + 32)

        def steps(eng, step, lags, count, unroll=2):
            top = max(lags)
            lo = -(-max(top, 2) // unroll) * unroll
            hi = lo + (count - lo) // unroll * unroll

            def live(t):
                return [0 <= t - g < count for g in lags]

            for t in range(lo):
                step(t, t % unroll, live(t))
            with eng.Fori(lo // unroll, hi // unroll) as i:
                for r in range(unroll):
                    step(i * unroll + r, r, [True] * len(lags))
            for t in range(hi, count + top):
                step(t, t % unroll, live(t))

        NORM, PREPARE, CONVOLVE, TO_ROWS, ROUTE = range(5)

        def landed(eng, ring, h, h4):
            eng.wait_ge(ring[h4], (h - h4) * 4 + 16)

        def fill_behind(eng, part):
            eng.wait_ge(s_tab, 1)
            for e in range(part, E, 3):
                at = eng.value_load(fill_at[0:1, e:e + 1], min_val=e * CAP, max_val=e * CAP + TOKENS)
                eng.dma_start(regions[bass.ds(at, P), :], filler[:, :]).then_inc(s_fill[part], 16)

        block = es.enter_context(nc.Block())

        @block.sync
        def _(sp):
            def load_x(h, q):
                after(sp, s_base, h - 3)
                after(sp, s_vcps, h - 3)
                sp.dma_start(xr[:, q, :], head_rows(x, h)).then_inc(s_x[q], 16)
                sp.dma_start(cr[:, q, :], head_rows(ctx, h)).then_inc(s_c[q], 16)

            load_x(0, 0)
            sp.wait_ge(s_kzero, 1)
            sp.dma_start(kin[:, P:], k).then_inc(s_kin, 16)
            sp.dma_start(bias_rows[:, :, :], bass.AP(tensor=fside.tensor, offset=0,
                                                     ap=[[NH, H], [0, B], [1, NH]])).then_inc(s_bias, 16)
            sp.dma_start(wg[:, :, :], w_gate.rearrange("(c p) e -> p c e", p=P)).then_inc(s_wg, 16)
            sp.wait_ge(s_kin, 16)
            sp.dma_start(kpad, kin[:, :]).then_inc(s_kpad, 16)
            sp.wait_ge(s_kpad, 16)
            for n in range(4):
                sp.dma_start(hank[:, n * (H // 4):(n + 1) * (H // 4), :], bass.AP(
                    tensor=kpad.tensor, offset=n * (H // 4) * (P + L) + 1,
                    ap=[[1, P], [P + L, H // 4], [1, L]])).then_inc(s_diag, 16)
                if n == 0:
                    sp.wait_ge(s_diag, 16)

            def step(t, q, live):
                norm, to_rows = live
                if norm and not (isinstance(t, int) and t == 0):
                    load_x(t, q)
                if to_rows:
                    h, r = t - TO_ROWS, (q - TO_ROWS) % 2
                    sp.wait_ge(s_xn, h + 1)
                    sp.dma_start(head_rows(out, h), xn[:, r, :]).then_inc(s_xst[r], 16)

            steps(sp, step, [NORM, TO_ROWS], H, 4)

            fill_behind(sp, 0)
            sp.wait_ge(s_tab, TABLE_STEPS)
            for n in range(H - 4, H):
                scattered(sp, n, n % 4)
            for part in range(3):
                sp.wait_ge(s_fill[part], len(range(part, E, 3)) * 16)
            sp.wait_ge(s_fillw, SPARE * 16)

            def tile(s, q, live):
                at = sp.value_load(tile_row[0:1, bass.ds(s, 1)], min_val=0, max_val=E * CAP + (SPARE - 1) * P)
                after(sp, s_meta, s - 1)
                after(sp, s_xTps, s - 1)
                sp.dma_start(xin[:, q, :], regions[bass.ds(at, P), :]).then_inc(s_xin[q], 16)

            steps(sp, tile, [0], TILES)
            for q in range(2):
                sp.wait_ge(s_add[q], (TILES + 1 - q) // 2 * 16)

        @block.gpsimd
        def _(pool):
            pool.memset(ones[:, :], 1.0)
            pool.memset(ident[:, :], 0.0)
            pool.memset(flip[:, :], 0.0)
            pool.memset(earlier[:, :], 1.0)
            pool.memset(same_b[:, :, :], 1.0)
            pool.memset(lower_e[:, :, :], 1.0)
            pool.memset(filler[:, 0:ID_COL], 0.0)
            pool.memset(filler[:, ID_COL:ROW], float(TOKENS)).then_inc(s_filler, 1)
            pool.memset(neg_half[:, :], -0.5)
            pool.memset(msum[:, :, :], 0.0)
            pool.memset(one_row[:, :], 1.0)
            pool.iota(region_i[:, :], [[CAP, E]], base=0, channel_multiplier=0)
            pool.iota(choice_i[:, :], [[1, TOPK]], base=0, channel_multiplier=0)
            pool.iota(head_i[:, :], [[NH, H]], base=0, channel_multiplier=0)
            pool.iota(tile_i[:, :], [[1, TILES]], base=0, channel_multiplier=0)
            pool.iota(pid_i[:, :], [[0, 1]], base=0, channel_multiplier=1).then_inc(s_consts, 1)
            pool.wait_ge(s_consts, 1)
            pool.affine_select(out=ident[:, :], in_=ident[:, :], compare_op=ALU.not_equal, fill=1.0,
                               base=0, pattern=[[-1, P]], channel_multiplier=1)
            pool.affine_select(out=flip[:, :], in_=flip[:, :], compare_op=ALU.not_equal, fill=1.0,
                               base=1 - P, pattern=[[1, P]], channel_multiplier=1)
            pool.affine_select(out=earlier[:, :], in_=earlier[:, :], compare_op=ALU.is_ge, fill=0.0,
                               base=-1, pattern=[[1, P]], channel_multiplier=-1)
            pool.affine_select(out=lower_e[:, :, :], in_=lower_e[:, :, :], compare_op=ALU.is_ge, fill=0.0,
                               base=-1, pattern=[[1, E], [-1, E]], channel_multiplier=0)
            pool.affine_select(out=same_b[:, :, :], in_=same_b[:, :, :], compare_op=ALU.is_ge, fill=0.0,
                               base=0, pattern=[[-NH, B], [0, NH]], channel_multiplier=1).then_inc(s_consts, 1)
            pool.wait_ge(s_consts, 2)
            pool.affine_select(out=same_b[:, :, :], in_=same_b[:, :, :], compare_op=ALU.is_ge, fill=0.0,
                               base=NH - 1, pattern=[[NH, B], [0, NH]], channel_multiplier=-1).then_inc(s_consts, 1)

            def step(t, q4, live):
                norm, prepare, to_rows, send = live
                q = q4 % 2
                r = 1 - q
                if prepare:
                    h, h4 = t - PREPARE, (q4 - PREPARE) % 4
                    pool.wait_ge(s_xhat, h + 1)
                    landed(pool, s_c, h, h4)
                    after(pool, s_skps, h - 1)
                    pool.tensor_tensor(u[:, r, :], xhat[:, r, :], cr[:, h4, :], ALU.mult).then_inc(s_u, 1)
                if to_rows:
                    h = t - TO_ROWS
                    pool.wait_ge(s_mv2a, h + 1)
                    pool.tensor_tensor(rstd2[:, r, :], ve2[:, r, :], neg_half[:, :], ALU.pow).then_inc(s_rstd2, 1)
                if prepare:
                    h = t - PREPARE
                    pool.wait_ge(s_vcT, h + 1)
                    after(pool, s_conv, (h - 1) * LB * NC)
                    for m in range(LB):
                        v = vcT[:, r, 0, m, :].rearrange("p (b i) -> p i b", i=NH)
                        c = vcT[:, r, 1, m, :].rearrange("p (b j) -> p b j", j=NH)
                        pool.tensor_tensor(kv[:, r, m],
                                           v.unsqueeze(3).to_broadcast([P, NH, B, NH]),
                                           c.unsqueeze(1).to_broadcast([P, NH, B, NH]),
                                           ALU.mult).then_inc(s_kv, 1)
                if norm:
                    h = t
                    pool.wait_ge(s_ve1, h + 1)
                    pool.tensor_tensor(rstd1[:, q, :], ve1[:, q, :], neg_half[:, :], ALU.pow).then_inc(s_rstd1, 1)
                if send:
                    h = t - ROUTE
                    scattered(pool, h - 4, q4)
                    pool.tensor_copy(rows[:, q4, :, ID_COL],
                                     out_row[:, bass.ds(h, 1)].to_broadcast([P, TOPK])).then_inc(s_id, 1)
                    wait_apart(pool, (s_id, h + 1), (s_dest, h + 1), (s_wt, h + 1), (s_rowB, h + 1))
                    for c in range(TOPK):
                        pool.indirect_dma_start(
                            out=regions, out_offset=bass.IndirectOffsetOnAxis(ap=dest[:, q4, c:c + 1], axis=0),
                            in_=rows[:, q4, c, :], in_offset=None).then_inc(s_scat[q4], 16)

            pool.wait_ge(s_setup, 9)
            steps(pool, step, [NORM, PREPARE, TO_ROWS, ROUTE], H, 4)
            fill_behind(pool, 2)
            for q in range(2):
                pool.wait_ge(s_xst[q], H // 2 * 16)

            def tile(s, q4, live):
                q = q4 % 2
                added = [] if isinstance(s, int) and s == 0 else [(s_add[1 - q], (s - 1 - (1 - q)) * 8 + 16)]
                wait_apart(pool, (s_ys, s + 1), (s_meta, s + 1), *added)
                pool.indirect_dma_start(
                    out=out_rows, out_offset=bass.IndirectOffsetOnAxis(ap=idx[q4][:, :], axis=0),
                    in_=ys[q][:, :], in_offset=None, bounds_check=TOKENS - 1, oob_is_err=False,
                    compute_op=ALU.add).then_inc(s_add[q], 16)

            steps(pool, tile, [0], TILES, 4)

        @block.scalar
        def _(act):
            for n in range(SPARE):
                if n == 0:
                    act.wait_ge(s_filler, 1)
                act.dma_start(regions[E * CAP + n * P:E * CAP + (n + 1) * P, :], filler[:, :]).then_inc(s_fillw, 16)
            act.wait_ge(s_bias_ps, 1)
            act.activation(bias_pp[:, :], mix_bank[:, 0:H], ACT.Copy).then_inc(s_bias_pp, 1)
            act.wait_ge(s_bias_pp, 1)
            act.wait_ge(s_consts, 3)

            def load_weights(e, part):
                if part == 0:
                    act.dma_start(W1[:, bass.ds(e, 1)].rearrange("p e c n -> p (e c) n"), bass.AP(
                        tensor=w1.tensor, offset=e * (L * INNER),
                        ap=[[INNER, P], [P * INNER, LB], [1, INNER]])).then_inc(s_w, 16)
                else:
                    act.dma_start(W3[:, bass.ds(e, 1)].rearrange("p e c n -> p (e c) n"), bass.AP(
                        tensor=w3.tensor, offset=e * (L * INNER),
                        ap=[[INNER, P], [P * INNER, LB], [1, INNER]])).then_inc(s_w, 16)
                    act.dma_start(W2[:, bass.ds(e, 1)].rearrange("p e c n -> p (e c) n"), bass.AP(
                        tensor=w2.tensor, offset=e * (L * INNER),
                        ap=[[L, P], [P * L, KB], [1, L]])).then_inc(s_w, 16)

            def step(t, q4, live):
                norm, prepare, to_rows, route = live
                q = q4 % 2
                r = 1 - q
                if prepare:
                    h, h4 = t - PREPARE, (q4 - PREPARE) % 4
                    act.wait_ge(s_rstd1, h + 1)
                    act.wait_ge(s_nm1, h + 1)
                    act.activation(nmr1[:, r, :], nm1[:, r, :], ACT.Copy, scale=rstd1[:, r, :]).then_inc(s_nmr1, 1)
                    act.wait_ge(s_nmr1, h + 1)
                    landed(act, s_x, h, h4)
                    after(act, s_vcps, h - 1)
                    after(act, s_u, h - 1)
                    act.activation(xhat[:, r, :], xr[:, h4, :], ACT.Identity, bias=nmr1[:, r, :],
                                   scale=rstd1[:, r, :]).then_inc(s_xhat, 1)
                    after(act, s_skps, h - 1)
                    act.activation(skip_mat[:, r, :], same_b[:, :, :].rearrange("p b j -> p (b j)"), ACT.Copy,
                                   scale=bias_pp[:, bass.ds(h, 1)]).then_inc(s_smat, 1)
                if route:
                    h = t - ROUTE
                    act.wait_ge(s_nb, h + 1)
                    act.activation(ex[:, :], th[:, q, :], ACT.Exp, bias=nbias[:, :], scale=SOFTCAP,
                                   accum_out=esum[:, :]).then_inc(s_ex, 1)
                if norm:
                    load_weights((t - q) // 2, q)
                if prepare:
                    h = t - PREPARE
                    act.wait_ge(s_vcps, h + 1)
                    after(act, s_z, (h - 1) * LB * NC)
                    after(act, s_kv, (h - 1) * LB)
                    act.activation(vcT[:, r].rearrange("p a m t -> p (a m t)"), vc_bank[:, :], ACT.Copy).then_inc(s_vcT, 1)
                if to_rows:
                    h, h4 = t - TO_ROWS, (q4 - TO_ROWS) % 4
                    act.wait_ge(s_nmr2, h + 1)
                    act.wait_ge(s_xn, h + 1)
                    scattered(act, h - 4, h4)
                    act.activation(rows[:, h4, 0, 0:L], xn[:, r, :], ACT.Identity, bias=nmr2[:, r, :],
                                   scale=rstd2[:, r, :]).then_inc(s_rowA, 1)
                    act.wait_ge(s_rowA, h + 1)
                    act.activation(rows[:, h4, 1, 0:L], rows[:, h4, 0, 0:L], ACT.Copy).then_inc(s_rowB, 1)
                if norm:
                    h = t
                    landed(act, s_x, h, q4)
                    act.activation(junk[:, :], xr[:, q4, :], ACT.Copy, accum_out=sum1[:, q, :]).then_inc(s_sum1, 1)
                    act.wait_ge(s_sum1, h + 1)
                    act.activation(nm1[:, q, :], sum1[:, q, :], ACT.Copy, scale=-1.0 / L).then_inc(s_nm1, 1)
                    act.wait_ge(s_nm1, h + 1)
                    act.activation(junk[:, :], xr[:, q4, :], ACT.Square, bias=nm1[:, q, :],
                                   accum_out=ssq1[:, q, :]).then_inc(s_ssq1, 1)
                if to_rows:
                    h = t - TO_ROWS
                    act.wait_ge(s_xT2ps, h + 1)
                    after(act, s_logit, h - 1)
                    act.activation(xT2[:, r].rearrange("p m t -> p (m t)"), gate_bank[:, 0:L], ACT.Copy).then_inc(s_xT2, 1)
                if norm:
                    h = t
                    act.wait_ge(s_ssq1, h + 1)
                    act.activation(ve1[:, q, :], ssq1[:, q, :], ACT.Copy, bias=LN_EPS, scale=1.0 / L).then_inc(s_ve1, 1)
                if to_rows:
                    h = t - TO_ROWS
                    act.wait_ge(s_logit, h + 1)
                    act.activation(th[:, r, :], gate_bank[:, L:L + E], ACT.Tanh, scale=1.0 / SOFTCAP).then_inc(s_th, 1)
                if prepare:
                    h = t - PREPARE
                    act.wait_ge(s_toepps, h + 1)
                    after(act, s_conv, (h - 1) * LB * NC)
                    act.activation(toep[:, r, :], vc_bank[:, 0:L], ACT.Copy).then_inc(s_toep, 1)

            steps(act, step, [NORM, PREPARE, TO_ROWS, ROUTE], H, 4)
            act.activation(silu0[:, :], neg_half[:, :], ACT.Silu)
            fill_behind(act, 1)

            def tile(s, q4, live):
                q = q4 % 2
                now_x, now_h, now_y = live
                if now_x:
                    act.wait_ge(s_xTps, s + 1)
                    after(act, s_h3, s - 1)
                    act.activation(xT[:, q].rearrange("p m t -> p (m t)"), xT_bank[:, 0:L], ACT.Copy).then_inc(s_xT, 1)
                if now_h:
                    n, r = s - 1, 1 - q
                    act.wait_ge(s_h1, n + 1)
                    after(act, s_gated, n - 1)
                    act.activation(act1[:, r, :], h1_bank[r][:, :], ACT.Silu).then_inc(s_act, 1)
                if now_y:
                    n = s - 2
                    act.wait_ge(s_y, n + 1)
                    act.wait_ge(s_meta, n + 1)
                    if not (isinstance(n, int) and n < 2):
                        loads(act, s_add, n - 2, q)
                    act.activation(ys[q][:, :], y_bank[q][:, 0:L], ACT.Copy,
                                   scale=wt[:, (q4 - 2) % 4, :]).then_inc(s_ys, 1)

            steps(act, tile, [0, 1, 2], TILES, 4)

        @block.vector
        def _(dve):
            dve.memset(kin[:, 0:P], 0.0).then_inc(s_kzero, 1)
            dve.wait_ge(s_consts, 3)
            dve.tensor_copy(region[:, :], region_i[:, :]).then_inc(s_setup, 1)
            dve.tensor_copy(choice[:, :], choice_i[:, :]).then_inc(s_setup, 1)
            dve.tensor_copy(head_f[:, :], head_i[:, :]).then_inc(s_setup, 1)
            dve.tensor_copy(tile_f[:, :], tile_i[:, :]).then_inc(s_setup, 1)
            dve.tensor_copy(pid_f[:, :], pid_i[:, :]).then_inc(s_setup, 1)
            dve.tensor_scalar(pid_b[:, :], pid_i[:, :], NH.bit_length() - 1, None,
                              ALU.logical_shift_right).then_inc(s_setup, 1)
            dve.wait_ge(s_setup, 6)
            dve.tensor_copy(pid_bf[:, :], pid_b[:, :]).then_inc(s_setup, 1)
            dve.wait_ge(s_setup, 7)
            dve.scalar_tensor_tensor(row0[:, :], pid_bf[:, :], float(D - NH), pid_f[:, :], ALU.mult,
                                     ALU.add).then_inc(s_setup, 1)
            dve.wait_ge(s_setup, 8)
            dve.tensor_scalar(out_row[:, :], head_f[:, :], row0[:, :], None, ALU.add).then_inc(s_setup, 1)

            def z_bank(h, q, m, c):
                n = (m * NC + c)
                dve.wait_ge(s_conv, h * (LB * NC) + n + 1)
                cb = vcT[:, q, 1, m, :].rearrange("p (b i) -> p i b", i=NH)[:, c * CH:(c + 1) * CH, :]
                dve.tensor_tensor(z[:, m, c * CH:(c + 1) * CH, :].rearrange("p i (b j) -> p i b j", b=B),
                                  conv_bank[m][c][:, :].rearrange("p (i b j) -> p i b j", i=CH, b=B),
                                  cb.unsqueeze(3).to_broadcast([P, CH, B, NH]), ALU.mult).then_inc(s_z, 1)

            def sum_i(h, q, m):
                dve.wait_ge(s_z, h * (LB * NC) + (m + 1) * NC)
                after(dve, s_mixps, h - 1)
                dve.tensor_reduce(mixT[:, q, m, :], z[:, m, :, :].rearrange("p i t -> p t i"), AX.X,
                                  ALU.add).then_inc(s_mixT, 1)

            def step(t, q4, live):
                prepare, convolve, to_rows, route = live
                q = q4 % 2
                r = 1 - q
                if route:
                    h = t - ROUTE
                    dve.wait_ge(s_th, h + 1)
                    dve.tensor_reduce(tmax[:, :], th[:, q, :], AX.X, ALU.max).then_inc(s_tmax, 1)
                    dve.wait_ge(s_tmax, h + 1)
                    dve.tensor_scalar(nbias[:, :], tmax[:, :], -SOFTCAP, None, ALU.mult).then_inc(s_nb, 1)
                if to_rows:
                    h = t - TO_ROWS
                    dve.wait_ge(s_mixps, h + 1)
                    dve.wait_ge(s_base, h + 1)
                    after(dve, s_rowA, h - 1)
                    if not (isinstance(h, int) and h < 2):
                        loads(dve, s_xst, h - 2, r)
                    dve.tensor_tensor(xn[:, r, :], mix_bank[:, 0:L], base[:, r, :], ALU.add).then_inc(s_xn, 1)
                    dve.wait_ge(s_xn, h + 1)
                    dve.bn_stats(st2[:, r, :], xn[:, r, :]).then_inc(s_st2, 1)
                    wait_apart(dve, (s_st2, h + 1))
                    dve.bn_aggr(mv2[:, r, :], st2[:, r, :]).then_inc(s_mv2, 1)
                    dve.wait_ge(s_mv2, h + 1)
                    dve.tensor_scalar(ve2[:, r, :], mv2[:, r, 1:2], LN_EPS, None, ALU.add).then_inc(s_mv2a, 1)
                if convolve:
                    z_bank(t - CONVOLVE, q, 0, 0)
                    z_bank(t - CONVOLVE, q, 0, 1)
                if to_rows:
                    h = t - TO_ROWS
                    dve.wait_ge(s_rstd2, h + 1)
                    dve.scalar_tensor_tensor(nmr2[:, r, :], mv2[:, r, 0:1], -1.0, rstd2[:, r, :],
                                             ALU.mult, ALU.mult).then_inc(s_nmr2, 1)
                if route:
                    h = t - ROUTE
                    dve.wait_ge(s_ex, h + 1)
                    dve.reciprocal(rsum[:, :], esum[:, :]).then_inc(s_rsum, 1)
                    dve.wait_ge(s_rsum, h + 1)
                    dve.tensor_scalar(prob[:, :], ex[:, :], rsum[:, :], None, ALU.mult).then_inc(s_prob, 1)
                    dve.wait_ge(s_prob, h + 1)
                    pf = prob[:, :].unsqueeze(1).to_broadcast([P, E, E])
                    pe = prob[:, :].unsqueeze(2).to_broadcast([P, E, E])
                    dve.tensor_tensor(eq[:, :, :], pf, pe, ALU.is_equal).then_inc(s_eq, 1)
                    dve.tensor_tensor(gt[:, :, :], pf, pe, ALU.is_gt).then_inc(s_gt, 1)
                    dve.wait_ge(s_eq, h + 1)
                    dve.tensor_tensor(eql[:, :, :], eq[:, :, :], lower_e[:, :, :], ALU.mult).then_inc(s_eql, 1)
                    dve.wait_ge(s_eql, h + 1)
                    dve.wait_ge(s_gt, h + 1)
                    dve.tensor_tensor(ahead[:, :, :], gt[:, :, :], eql[:, :, :], ALU.add).then_inc(s_ahead, 1)
                    dve.wait_ge(s_ahead, h + 1)
                    dve.tensor_reduce(order[:, :], ahead[:, :, :], AX.X, ALU.add).then_inc(s_order, 1)
                    dve.wait_ge(s_order, h + 1)
                    after(dve, s_rankps, h)
                    dve.tensor_scalar(mask[:, :], order[:, :], float(TOPK), None, ALU.is_lt).then_inc(s_mask, 1)
                if convolve:
                    sum_i(t - CONVOLVE, q, 0)
                if prepare:
                    h, h4 = t - PREPARE, (q4 - PREPARE) % 4
                    landed(dve, s_c, h, h4)
                    landed(dve, s_x, h, h4)
                    dve.wait_ge(s_skps, h + 1)
                    dve.tensor_tensor(skip[:, :], skip_bank[:, 0:L], cr[:, h4, :], ALU.mult).then_inc(s_skip, 1)
                if convolve:
                    z_bank(t - CONVOLVE, q, 1, 0)
                if prepare:
                    h, h4 = t - PREPARE, (q4 - PREPARE) % 4
                    dve.wait_ge(s_skip, h + 1)
                    dve.tensor_tensor(base[:, r, :], skip[:, :], xr[:, h4, :], ALU.add).then_inc(s_base, 1)
                if convolve:
                    z_bank(t - CONVOLVE, q, 1, 1)
                if route:
                    h = t - ROUTE
                    dve.tensor_tensor(hot[:, :, :], order[:, :].unsqueeze(1).to_broadcast([P, TOPK, E]),
                                      choice[:, :].unsqueeze(2).to_broadcast([P, TOPK, E]),
                                      ALU.is_equal).then_inc(s_hot, 1)
                    dve.wait_ge(s_mask, h + 1)
                    dve.tensor_tensor(msum[:, 1 - q, :], msum[:, q, :], mask[:, :], ALU.add).then_inc(s_msum, 1)
                    dve.wait_ge(s_hot, h + 1)
                    dve.tensor_tensor(hotp[:, :, :], hot[:, :, :],
                                      prob[:, :].unsqueeze(1).to_broadcast([P, TOPK, E]), ALU.mult).then_inc(s_hotp, 1)
                if convolve:
                    sum_i(t - CONVOLVE, q, 1)
                if route:
                    h = t - ROUTE
                    dve.wait_ge(s_rankps, h + 1)
                    dve.tensor_tensor(pos[:, :], mix_bank[:, L:L + E], region[:, :], ALU.add).then_inc(s_pos, 1)
                    dve.wait_ge(s_hotp, h + 1)
                    dve.tensor_reduce(rows[:, q4, :, W_COL], hotp[:, :, :], AX.X, ALU.add).then_inc(s_wt, 1)
                    dve.wait_ge(s_pos, h + 1)
                    dve.tensor_tensor(hpos[:, :, :], hot[:, :, :],
                                      pos[:, :].unsqueeze(1).to_broadcast([P, TOPK, E]), ALU.mult).then_inc(s_hpos, 1)
                    dve.wait_ge(s_hpos, h + 1)
                    dve.tensor_reduce(destf[:, :], hpos[:, :, :], AX.X, ALU.add).then_inc(s_destf, 1)
                    dve.wait_ge(s_destf, h + 1)
                    dve.tensor_copy(dest[:, q4, :], destf[:, :]).then_inc(s_dest, 1)

            steps(dve, step, [PREPARE, CONVOLVE, TO_ROWS, ROUTE], H, 4)

            chain = [0]

            def link(ins):
                ins.then_inc(s_tab, 1)
                chain[0] += 1
                dve.wait_ge(s_tab, chain[0])

            dve.wait_ge(s_cnt, 1)
            cnt = skip_bank[0:1, 0:E]
            link(dve.tensor_tensor(fill_at[:, :], cnt, region[0:1, :], ALU.add))
            link(dve.tensor_scalar(nt_i[:, :], cnt, float(P - 1), None, ALU.add))
            link(dve.tensor_scalar(nt_s[:, :], nt_i[:, :], P.bit_length() - 1, None, ALU.logical_shift_right))
            link(dve.tensor_copy(nt[:, :], nt_s[:, :]))
            link(dve.tensor_tensor_scan(upto[:, :], one_row[:, :], nt[:, :], 0.0, ALU.mult, ALU.add))
            link(dve.tensor_tensor(past[:, :, :], tile_f[:, :].unsqueeze(2).to_broadcast([1, TILES, E]),
                                   upto[:, :].unsqueeze(1).to_broadcast([1, TILES, E]), ALU.is_ge))
            link(dve.tensor_tensor(past_nt[:, :, :], past[:, :, :],
                                   nt[:, :].unsqueeze(1).to_broadcast([1, TILES, E]), ALU.mult))
            link(dve.tensor_reduce(eid[:, :], past[:, :, :], AX.X, ALU.add))
            link(dve.tensor_reduce(first[:, :], past_nt[:, :, :], AX.X, ALU.add))
            link(dve.tensor_scalar(tile_expert[:, :], eid[:, :], float(E - 1), None, ALU.min))
            link(dve.tensor_tensor(inside[:, :], tile_f[:, :], first[:, :], ALU.subtract))
            link(dve.tensor_scalar(reg_at[:, :], eid[:, :], float(CAP), None, ALU.mult))
            link(dve.tensor_scalar(first[:, :], inside[:, :], float(P), None, ALU.mult))
            link(dve.tensor_tensor(tile_row[:, :], first[:, :], reg_at[:, :], ALU.add))
            assert chain[0] == TABLE_STEPS

            def tile(s, q4, live):
                q = q4 % 2
                now_meta, now_h, now_y = live
                if now_y:
                    n = s - 2
                    dve.wait_ge(s_gTps, n + 1)
                    after(dve, s_y, n - 1)
                    dve.tensor_copy(gT[:, q].rearrange("p m t -> p (m t)"), gT_bank[:, :]).then_inc(s_gT, 1)
                if now_meta:
                    loads(dve, s_xin, s, q)
                    if not (isinstance(s, int) and s < 4):
                        loads(dve, s_add, s - 4, q)
                    dve.tensor_copy(wt[:, q4, :], xin[:, q, W_COL:W_COL + 1])
                    dve.tensor_copy(idx[q4][:, :], xin[:, q, ID_COL:ROW]).then_inc(s_meta, 1)
                if now_h:
                    n, r = s - 1, 1 - q
                    dve.wait_ge(s_act, n + 1)
                    dve.wait_ge(s_h3, n + 1)
                    after(dve, s_gTps, n - 1)
                    dve.tensor_tensor(gated[:, r, :], act1[:, r, :], h3_bank[r][:, :], ALU.mult).then_inc(s_gated, 1)

            steps(dve, tile, [0, 1, 2], TILES, 4)

        @block.tensor
        def _(pe):
            pe.wait_ge(s_consts, 3)
            pe.wait_ge(s_bias, 16)
            pe.transpose(mix_bank[:, 0:H], bias_rows[:, :, :].rearrange("h b i -> h (b i)"),
                         ident[0:H, 0:H]).then_inc(s_bias_ps, 1)
            pe.wait_ge(s_wg, 16)
            pe.wait_ge(s_bias_pp, 1)

            def conv(h, q, m):
                for c in range(NC):
                    after(pe, s_z, (h - 1) * (LB * NC) + m * NC + c + 1)
                    for n in range(m + 1):
                        mm = pe.matmul(conv_bank[m][c][:, :],
                                       toep[:, q, (m - n) * P:(m - n + 1) * P],
                                       kv[:, q, n, c * CH:(c + 1) * CH].rearrange("p i b j -> p (i b j)"),
                                       start=(n == 0), stop=(n == m))
                    mm.then_inc(s_conv, 1)

            def step(t, q4, live):
                prepare, convolve, to_rows, route = live
                q = q4 % 2
                r = 1 - q
                if to_rows:
                    h = t - TO_ROWS
                    pe.wait_ge(s_mixT, (h + 1) * LB)
                    after(pe, s_xn, h)
                    after(pe, s_pos, h - 1)
                    for m in range(LB):
                        mm = pe.transpose(mix_bank[:, m * P:(m + 1) * P], mixT[:, r, m, :], ident[:, :])
                    mm.then_inc(s_mixps, 1)
                if convolve:
                    h = t - CONVOLVE
                    pe.wait_ge(s_kv, (h + 1) * LB)
                    pe.wait_ge(s_toep, h + 1)
                    conv(h, q, 0)
                if prepare:
                    h, h4 = t - PREPARE, (q4 - PREPARE) % 4
                    pe.wait_ge(s_xhat, h + 1)
                    landed(pe, s_c, h, h4)
                    after(pe, s_toep, h)
                    for a, src in ((0, xhat[:, r, :]), (1, cr[:, h4, :])):
                        for m in range(LB):
                            mm = pe.transpose(vc_bank[:, (a * LB + m) * P:(a * LB + m + 1) * P],
                                              src[:, m * P:(m + 1) * P], ident[:, :])
                    mm.then_inc(s_vcps, 1)
                    pe.wait_ge(s_u, h + 1)
                    after(pe, s_skip, h)
                    pe.wait_ge(s_smat, h + 1)
                    pe.matmul(skip_bank[:, 0:L], skip_mat[:, r, :], u[:, r, :], start=True, stop=True).then_inc(s_skps, 1)
                if convolve:
                    conv(t - CONVOLVE, q, 1)
                if route:
                    h = t - ROUTE
                    pe.wait_ge(s_mask, h + 1)
                    after(pe, s_msum, h)
                    if to_rows:
                        pe.wait_ge(s_xn, h + 2)
                    after(pe, s_pos, h)
                    pe.matmul(mix_bank[:, L:L + E], earlier[:, :], mask[:, :], start=True, stop=False)
                    pe.matmul(mix_bank[:, L:L + E], ones[:, :], msum[:, q, :], start=False, stop=True).then_inc(s_rankps, 1)
                if to_rows:
                    h, h4 = t - TO_ROWS, (q4 - TO_ROWS) % 4
                    pe.wait_ge(s_rowA, h + 1)
                    after(pe, s_th, h)
                    for m in range(LB):
                        mm = pe.transpose(gate_bank[:, m * P:(m + 1) * P], rows[:, h4, 0, m * P:(m + 1) * P], ident[:, :])
                    mm.then_inc(s_xT2ps, 1)
                if prepare:
                    h = t - PREPARE
                    pe.wait_ge(s_vcT, h + 1)
                    if isinstance(h, int) and h < 4:
                        pe.wait_ge(s_diag, 16 if h == 0 else 4 * 16)
                    pe.matmul(vc_bank[:, 0:L], flip[:, :], hank[:, bass.ds(h, 1), :].rearrange("p a l -> p (a l)"),
                              start=True, stop=True).then_inc(s_toepps, 1)
                if to_rows:
                    h = t - TO_ROWS
                    pe.wait_ge(s_xT2, h + 1)
                    for m in range(LB):
                        mm = pe.matmul(gate_bank[:, L:L + E], xT2[:, r, m, :], wg[:, m, :],
                                       start=(m == 0), stop=(m == LB - 1))
                    mm.then_inc(s_logit, 1)

            steps(pe, step, [PREPARE, CONVOLVE, TO_ROWS, ROUTE], H, 4)
            pe.wait_ge(s_msum, H)
            pe.wait_ge(s_pos, H)
            pe.matmul(skip_bank[:, 0:E], ones[:, :], msum[:, H % 2, :], start=True, stop=True).then_inc(s_cnt, 1)

            pe.wait_ge(s_w, 3 * E * 16)
            pe.wait_ge(s_tab, TABLE_STEPS)
            pe.wait_ge(s_z, H * LB * NC)

            def tile(s, q4, live):
                q = q4 % 2
                now_x, now_h, now_y = live
                if now_x:
                    loads(pe, s_xin, s, q)
                    after(pe, s_xT, s)
                    for m in range(LB):
                        mm = pe.transpose(xT_bank[:, m * P:(m + 1) * P], xin[:, q, m * P:(m + 1) * P], ident[:, :])
                    mm.then_inc(s_xTps, 1)
                if now_h:
                    n, r = s - 1, 1 - q
                    e = pe.value_load(tile_expert[0:1, bass.ds(n, 1)], min_val=0, max_val=E - 1)
                    pe.wait_ge(s_xT, n + 1)
                    after(pe, s_act, n - 1)
                    for m in range(LB):
                        mm = pe.matmul(h1_bank[r][:, :], xT[:, r, m, :],
                                       W1[:, bass.ds(e, 1), m, :], start=(m == 0), stop=(m == LB - 1))
                    mm.then_inc(s_h1, 1)
                if now_y:
                    n = s - 2
                    pe.wait_ge(s_gated, n + 1)
                    after(pe, s_gT, n)
                    for m in range(KB):
                        mm = pe.transpose(gT_bank[:, m * P:(m + 1) * P], gated[:, q, m * P:(m + 1) * P], ident[:, :])
                    mm.then_inc(s_gTps, 1)
                if now_h:
                    n, r = s - 1, 1 - q
                    after(pe, s_gated, n - 1)
                    for m in range(LB):
                        mm = pe.matmul(h3_bank[r][:, :], xT[:, r, m, :],
                                       W3[:, bass.ds(e, 1), m, :], start=(m == 0), stop=(m == LB - 1))
                    mm.then_inc(s_h3, 1)
                if now_y:
                    n = s - 2
                    e = pe.value_load(tile_expert[0:1, bass.ds(n, 1)], min_val=0, max_val=E - 1)
                    pe.wait_ge(s_gT, n + 1)
                    after(pe, s_ys, n - 1)
                    for m in range(KB):
                        mm = pe.matmul(y_bank[q][:, 0:L], gT[:, q, m, :],
                                       W2[:, bass.ds(e, 1), m, :], start=(m == 0), stop=(m == KB - 1))
                    mm.then_inc(s_y, 1)

            steps(pe, tile, [0, 1, 2], TILES, 4)


_INS = ['x', 'fside_S2_0', 'ctx_2048', 'L0_xattn_k', 'L0_ffn_w_gate', 'L0_ffn_w1', 'L0_ffn_w3', 'L0_ffn_w2']
_OUTS = [((16, 128, 256), 'float32')]


def kernel(**inputs):
    import numpy as _np
    import concourse.bacc as _bacc
    from concourse import mybir as _mybir
    from concourse.bass_utils import run_bass_kernel_spmd as _run

    nc = _bacc.Bacc("TRN2", target_bir_lowering=False, num_devices=1)
    arrays, args = {}, []
    for name in _INS:
        a = _np.ascontiguousarray(inputs[name])
        arrays[f"in_{name}_dram"] = a
        args.append(nc.dram_tensor(f"in_{name}_dram", a.shape, _mybir.dt.from_np(a.dtype), kind="ExternalInput").ap())
    for i, (shape, dtype) in enumerate(_OUTS):
        dt = _mybir.dt.from_np(_np.dtype(dtype))
        args.append(nc.dram_tensor(f"out_{i}_dram", shape, dt, kind="ExternalOutput").ap())
    xattn_ffn_kernel(nc, *args)
    r = _run(nc, [arrays], core_ids=[0])
    got = tuple(r.results[0][f"out_{i}_dram"] for i in range(len(_OUTS)))
    return got[0]
```

```python
from contextlib import ExitStack

import concourse.bass as bass
from concourse import mybir

P = 128
F32 = mybir.dt.float32
F32R = mybir.dt.float32r
BF16 = mybir.dt.bfloat16
I32 = mybir.dt.int32
ALU = mybir.AluOpType
ACT = mybir.ActivationFunctionType
AX = mybir.AxisListType

LN_EPS = 1e-5
SOFTCAP = 30.0
TOPK = 2


def xattn_ffn_kernel(nc, x, fside, ctx, k, w_gate, w1, w3, w2, out):
    B, D, L = x.shape
    H = k.shape[0]
    NH = D // H
    E = w_gate.shape[1]
    INNER = w1.shape[2]
    LB = L // P
    KB = INNER // P
    TOKENS = B * D
    CAP = TOKENS + P
    TILES = (TOPK * TOKENS + E * (P - 1)) // P
    SPARE = TILES - TOPK * TOKENS // P
    ROW = L + 2
    W_COL, ID_COL = L, L + 1
    RANKS = L + E
    CH = 512 // P
    NC = NH // CH
    assert B * NH == P and LB == 2 and NC == 2 and KB * P == 512 and H % 2 == 0

    kpad = nc.dram_tensor("kpad", (H, P + L), F32, kind="Internal").ap()
    regions = nc.dram_tensor("regions", (E * CAP + SPARE * P, ROW), F32, kind="Internal").ap()
    out_rows = out.rearrange("b d l -> (b d) l")

    def head_rows(t, h):
        return bass.AP(tensor=t.tensor, offset=h * (NH * L), ap=[[D * L, B], [L, NH], [1, L]])

    with ExitStack() as es:
        def sb(name, shape, dt=F32, scope=es):
            return scope.enter_context(nc.sbuf_tensor(name, shape, dt))

        def sem(name):
            return es.enter_context(nc.semaphore(name))

        def sems(name, n=2):
            return [sem(f"{name}{i}") for i in range(n)]

        ident = sb("ident", [P, P])
        ones = sb("ones", [P, P])
        earlier = sb("earlier", [P, P], BF16)
        ones16 = sb("ones16", [P, P], BF16)
        same_b = sb("same_b", [P, B, NH])
        skip_mat = sb("skip_mat", [P, 2, P])
        bias_rows = sb("bias_rows", [H, B, NH])
        bias_pp = sb("bias_pp", [P, H])
        kzero = sb("kzero", [H, P])
        region_i = sb("region_i", [P, E], I32)
        region = sb("region", [P, E])
        expert_i = sb("expert_i", [P, E], I32)
        expert = sb("expert", [P, E])
        pid_i = sb("pid_i", [P, 1], I32)
        pid_b = sb("pid_b", [P, 1], I32)
        pid_f = sb("pid_f", [P, 1])
        pid_bf = sb("pid_bf", [P, 1])
        head_i = sb("head_i", [P, H], I32)
        head_f = sb("head_f", [P, H])
        row0 = sb("row0", [P, 1])
        out_row = sb("out_row", [P, H])
        filler = sb("filler", [P, ROW])
        neg_half = sb("neg_half", [P, 1])
        wg = sb("wg", [P, LB, E])
        silu0 = sb("silu0", [P, 1])
        W2 = sb("W2", [P, E, KB, L])
        flip = sb("flip", [P, P])
        sum1 = sb("sum1", [P, 2, 1])
        nm1 = sb("nm1", [P, 2, 1])
        ssq1 = sb("ssq1", [P, 2, 1])
        junk = sb("junk", [P, L])
        ve1 = sb("ve1", [P, 2, 1])
        nmr1 = sb("nmr1", [P, 2, 1])
        rstd1 = sb("rstd1", [P, 2, 1])
        skip = sb("skip", [P, L])
        xn = sb("xn", [P, 2, L])
        st2 = sb("st2", [P, 2, 6])
        mv2 = sb("mv2", [P, 2, 2])
        ve2 = sb("ve2", [P, 2, 1])
        nm2 = sb("nm2", [P, 2, 1])
        nmr2 = sb("nmr2", [P, 2, 1])
        rstd2 = sb("rstd2", [P, 2, 1])
        rows = sb("rows", [P, 4, TOPK, ROW])
        xT2 = sb("xT2", [P, 2, LB, P])
        th = sb("th", [P, 2, E])
        tmax = sb("tmax", [P, 2])
        nbias = sb("nbias", [P, 2])
        ex = sb("ex", [P, 2, E])
        esum = sb("esum", [P, 2])
        rsum = sb("rsum", [P, 2])
        prob = sb("prob", [P, 2, E])
        best = sb("best", [P, 2, 8])
        best_at = sb("best_at", [P, 2, 8], mybir.dt.uint32)
        hot = sb("hot", [P, 2, TOPK, E])
        mask = sb("mask", [P, 2, E], BF16)
        msum = sb("msum", [P, 2, E])
        msum_a = sb("msum_a", [P, E])
        pos = sb("pos", [P, 2, E])
        hpos = sb("hpos", [P, 2, TOPK, E])
        destf = sb("destf", [P, 2, TOPK])
        dest = sb("dest", [P, 4, TOPK], I32)
        fill_at = sb("fill_at", [1, E], I32)
        nt_i = sb("nt_i", [1, E], I32)
        nt_s = sb("nt_s", [1, E], I32)
        nt = sb("nt", [1, E])
        one_row = sb("one_row", [1, E])
        upto = sb("upto", [1, E])
        tile_i = sb("tile_i", [1, TILES], I32)
        tile_f = sb("tile_f", [1, TILES])
        past = sb("past", [1, TILES, E])
        past_nt = sb("past_nt", [1, TILES, E])
        eid = sb("eid", [1, TILES])
        first = sb("first", [1, TILES])
        inside = sb("inside", [1, TILES])
        reg_at = sb("reg_at", [1, TILES])
        tile_row = sb("tile_row", [1, TILES], I32)
        tile_expert = sb("tile_expert", [1, TILES], I32)
        xin = sb("xin", [P, 2, ROW])
        xTh = sb("xTh", [P, 2, LB, P], F32R)
        act1 = sb("act1", [P, 2, INNER])
        gated = sb("gated", [P, 2, INNER])
        gT = sb("gT", [P, 2, KB, P])
        ys = [sb(f"ys{q}", [P, L]) for q in range(2)]
        idx = [sb(f"idx{q}", [P, 1], I32) for q in range(4)]
        wt = sb("wt", [P, 4, 1])

        with ExitStack() as plain, ExitStack() as mixing:
            W13 = sb("W13", [P, E, 2, LB, INNER], scope=plain)
            hank = sb("hank", [P, H, L], scope=mixing)
            kv = sb("kv", [P, 2, LB, NH, B, NH], scope=mixing)
            z = sb("z", [P, LB, NH, P], scope=mixing)
            vcT = sb("vcT", [P, 4, 2, LB, P], scope=mixing)
            xr = sb("xr", [P, 4, L], scope=mixing)
            cr = sb("cr", [P, 4, L], scope=mixing)
            xhat = sb("xhat", [P, 2, L], scope=mixing)
            u = sb("u", [P, 2, L], scope=mixing)
            toep = sb("toep", [P, 2, L], scope=mixing)
            mixT = sb("mixT", [P, 2, LB, P], scope=mixing)
            base = sb("base", [P, 2, L], scope=mixing)
        W13l = sb("W13l", [P, E, 2, LB, INNER], F32R)
        W13h = sb("W13h", [P, E, 2, LB, INNER], F32R)
        xTl = sb("xTl", [P, 2, LB, P], F32R)

        bank = [es.enter_context(nc.psum_tensor(f"bank{i}", [P, 512], F32)) for i in range(8)]
        conv_bank = [[bank[2 * m + c] for c in range(NC)] for m in range(LB)]
        vc_bank = bank[4]
        mix_bank = bank[5]
        skip_bank = bank[6]
        gate_bank = bank[7]
        h1_bank, h3_bank = bank[0:2], bank[2:4]
        xT_bank, gT_bank = bank[4], bank[5]
        y_bank = bank[6:8]

        s_consts = sem("s_consts")
        s_setup = sem("s_setup")
        s_bias = sem("s_bias")
        s_bias_ps = sem("s_bias_ps")
        s_bias_pp = sem("s_bias_pp")
        s_filler = sem("s_filler")
        s_kzero = sem("s_kzero")
        s_kpad = sem("s_kpad")
        s_wg = sem("s_wg")
        s_w = sem("s_w")
        s_diag = sem("s_diag")
        s_toepps = sem("s_toepps")
        s_toep = sem("s_toep")
        s_x, s_c = sems("s_x", 4), sems("s_c", 4)
        s_sum1, s_nm1, s_ssq1, s_ve1 = sem("s_sum1"), sem("s_nm1"), sem("s_ssq1"), sem("s_ve1")
        s_rstd1, s_nmr1, s_xhat = sem("s_rstd1"), sem("s_nmr1"), sem("s_xhat")
        s_st2 = sem("s_st2")
        s_u = sem("s_u")
        s_smat = sem("s_smat")
        s_vcps = sem("s_vcps")
        s_vcT = sem("s_vcT")
        s_kv = sem("s_kv")
        s_conv = sem("s_conv")
        s_z = sem("s_z")
        s_mixT = sem("s_mixT")
        s_mixps = sem("s_mixps")
        s_skps = sem("s_skps")
        s_skip, s_base = sem("s_skip"), sem("s_base")
        s_xn, s_mv2, s_rstd2, s_ve2 = sem("s_xn"), sem("s_mv2"), sem("s_rstd2"), sem("s_ve2")
        s_xst = sems("s_xst")
        s_rowA, s_rowB = sem("s_rowA"), sem("s_rowB")
        s_xT2ps, s_xT2 = sem("s_xT2ps"), sem("s_xT2")
        s_logit, s_th = sem("s_logit"), sem("s_th")
        s_tmax, s_nb, s_ex = sem("s_tmax"), sem("s_nb"), sem("s_ex")
        s_rsum, s_prob = sem("s_rsum"), sem("s_prob")
        s_best, s_best_at = sem("s_best"), sem("s_best_at")
        s_hot, s_mask = sem("s_hot"), sem("s_mask")
        s_wt, s_msum_a, s_msum, s_rankps = sem("s_wt"), sem("s_msum_a"), sem("s_msum"), sem("s_rankps")
        s_pos, s_hpos, s_destf, s_dest = sem("s_pos"), sem("s_hpos"), sem("s_destf"), sem("s_dest")
        s_id = sem("s_id")
        s_scat = sems("s_scat", 4)
        s_nm2, s_nmr2 = sem("s_nm2"), sem("s_nmr2")
        s_fillw = sem("s_fillw")
        s_cnt = sem("s_cnt")
        s_tab = sem("s_tab")
        s_fill = sems("s_fill")
        s_xin = sems("s_xin")
        s_high = sem("s_high")
        s_low = sem("s_low")
        s_xTps, s_xT, s_xTl = sem("s_xTps"), sem("s_xT"), sem("s_xTl")
        s_h1, s_h3 = sem("s_h1"), sem("s_h3")
        s_act, s_gated = sem("s_act"), sem("s_gated")
        s_gTps, s_gT = sem("s_gTps"), sem("s_gT")
        s_y, s_ys, s_meta = sem("s_y"), sem("s_ys"), sem("s_meta")
        s_add = sems("s_add")

        s_apart = {nc.vector.engine: sem("s_apart_vector"), nc.gpsimd.engine: sem("s_apart_pool")}

        TABLE_STEPS = 14

        def after(eng, s, n):
            if not (isinstance(n, int) and n <= 0):
                eng.wait_ge(s, n)

        def wait_apart(eng, *waits):
            for s, n in waits:
                eng.wait_ge(s, n)
            eng.sem_inc(s_apart[eng.engine], 1)

        def loads(eng, pair, n, q):
            after(eng, pair[q], (n - q) * 8 + 16)

        def scattered(eng, h, h4):
            if not (isinstance(h, int) and h < 0):
                eng.wait_ge(s_scat[h4], (h - h4) * 8 + 32)

        def steps(eng, step, lags, count, unroll=2):
            top = max(lags)
            lo = -(-max(top + 1, 2) // unroll) * unroll
            hi = lo + (count - lo) // unroll * unroll

            def live(t):
                return [0 <= t - g < count for g in lags]

            for t in range(lo):
                step(t, t % unroll, live(t))
            with eng.Fori(lo // unroll, hi // unroll) as i:
                for r in range(unroll):
                    step(i * unroll + r, r, [True] * len(lags))
            for t in range(hi, count + top):
                step(t, t % unroll, live(t))

        NORM, PREPARE, CONVOLVE, TO_ROWS, ROUTE, PLACE, SEND = range(7)

        def landed(eng, ring, h, h4):
            eng.wait_ge(ring[h4], (h - h4) * 4 + 16)

        def fill_behind(eng, part):
            eng.wait_ge(s_tab, 1)
            for e in range(part, E, 2):
                at = eng.value_load(fill_at[0:1, e:e + 1], min_val=e * CAP, max_val=e * CAP + TOKENS)
                eng.dma_start(regions[bass.ds(at, P), :], filler[:, :]).then_inc(s_fill[part], 16)

        CHUNKS = 2 * E

        def high_chunks(act, chunks):
            for n in chunks:
                act.activation(W13h[:, n // 2, n % 2], W13[:, n // 2, n % 2], ACT.Copy).then_inc(s_high, 1)

        def low_chunks(eng, chunks):
            for n in chunks:
                eng.wait_ge(s_high, n + 1)
                eng.tensor_tensor(W13l[:, n // 2, n % 2], W13[:, n // 2, n % 2], W13h[:, n // 2, n % 2].bitcast(F32),
                                  ALU.subtract).then_inc(s_low, 1)

        block = es.enter_context(nc.Block())

        @block.sync
        def _(sp):
            def load_x(h, q):
                after(sp, s_base, h - 3)
                after(sp, s_vcps, h - 3)
                sp.dma_start(xr[:, q, :], head_rows(x, h)).then_inc(s_x[q], 16)
                sp.dma_start(cr[:, q, :], head_rows(ctx, h)).then_inc(s_c[q], 16)

            load_x(0, 0)
            sp.dma_start(kpad[:, P:], k).then_inc(s_kpad, 16)
            sp.wait_ge(s_kzero, 1)
            sp.dma_start(kpad[:, 0:P], kzero[:, :]).then_inc(s_kpad, 16)
            sp.dma_start(bias_rows[:, :, :], bass.AP(tensor=fside.tensor, offset=0,
                                                     ap=[[NH, H], [0, B], [1, NH]])).then_inc(s_bias, 16)
            sp.dma_start(wg[:, :, :], w_gate.rearrange("(c p) e -> p c e", p=P)).then_inc(s_wg, 16)
            load_x(1, 1)
            sp.wait_ge(s_kpad, 2 * 16)
            for n in range(4):
                sp.dma_start(hank[:, n * (H // 4):(n + 1) * (H // 4), :], bass.AP(
                    tensor=kpad.tensor, offset=n * (H // 4) * (P + L) + 1,
                    ap=[[1, P], [P + L, H // 4], [1, L]])).then_inc(s_diag, 16)
                if n == 0:
                    load_x(2, 2)
                    load_x(3, 3)
                    sp.wait_ge(s_diag, 16)

            for n in range(SPARE):
                if n == 0:
                    sp.wait_ge(s_filler, 1)
                sp.dma_start(regions[E * CAP + n * P:E * CAP + (n + 1) * P, :], filler[:, :]).then_inc(s_fillw, 16)

            def load_weights(e, part):
                if part == 0:
                    sp.dma_start(W13[:, bass.ds(e, 1), 0].rearrange("p e c n -> p (e c) n"), bass.AP(
                        tensor=w1.tensor, offset=e * (L * INNER),
                        ap=[[INNER, P], [P * INNER, LB], [1, INNER]])).then_inc(s_w, 16)
                else:
                    sp.dma_start(W13[:, bass.ds(e, 1), 1].rearrange("p e c n -> p (e c) n"), bass.AP(
                        tensor=w3.tensor, offset=e * (L * INNER),
                        ap=[[INNER, P], [P * INNER, LB], [1, INNER]])).then_inc(s_w, 16)
                    sp.dma_start(W2[:, bass.ds(e, 1)].rearrange("p e c n -> p (e c) n"), bass.AP(
                        tensor=w2.tensor, offset=e * (L * INNER),
                        ap=[[L, P], [P * L, KB], [1, L]])).then_inc(s_w, 16)

            def step(t, q, live):
                norm, to_rows = live
                if norm:
                    if not (isinstance(t, int) and t < 4):
                        load_x(t, q)
                    load_weights((t - q % 2) // 2, q % 2)
                if to_rows:
                    h, r = t - TO_ROWS, (q - TO_ROWS) % 2
                    sp.wait_ge(s_xn, h + 1)
                    sp.dma_start(head_rows(out, h), xn[:, r, :]).then_inc(s_xst[r], 16)

            steps(sp, step, [NORM, TO_ROWS], H, 4)

            fill_behind(sp, 0)
            sp.wait_ge(s_tab, TABLE_STEPS)
            for n in range(H - 4, H):
                scattered(sp, n, n % 4)
            for part in range(2):
                sp.wait_ge(s_fill[part], len(range(part, E, 2)) * 16)
            sp.wait_ge(s_fillw, SPARE * 16)

            def tile(s, q, live):
                at = sp.value_load(tile_row[0:1, bass.ds(s, 1)], min_val=0, max_val=E * CAP + (SPARE - 1) * P)
                after(sp, s_meta, s - 1)
                after(sp, s_xTps, s - 1)
                sp.dma_start(xin[:, q, :], regions[bass.ds(at, P), :]).then_inc(s_xin[q], 16)

            steps(sp, tile, [0], TILES)
            for q in range(2):
                sp.wait_ge(s_add[q], (TILES + 1 - q) // 2 * 16)

        @block.gpsimd
        def _(pool):
            pool.memset(ones[:, :], 1.0)
            pool.memset(ident[:, :], 0.0)
            pool.memset(flip[:, :], 0.0)
            pool.memset(earlier[:, :], 1.0)
            pool.memset(ones16[:, :], 1.0)
            pool.memset(same_b[:, :, :], 1.0)
            pool.memset(filler[:, 0:ID_COL], 0.0)
            pool.memset(filler[:, ID_COL:ROW], float(TOKENS)).then_inc(s_filler, 1)
            pool.memset(neg_half[:, :], -0.5)
            pool.memset(msum[:, :, :], 0.0)
            pool.memset(one_row[:, :], 1.0)
            pool.iota(region_i[:, :], [[CAP, E]], base=0, channel_multiplier=0)
            pool.iota(expert_i[:, :], [[1, E]], base=0, channel_multiplier=0)
            pool.iota(head_i[:, :], [[NH, H]], base=0, channel_multiplier=0)
            pool.iota(tile_i[:, :], [[1, TILES]], base=0, channel_multiplier=0)
            pool.iota(pid_i[:, :], [[0, 1]], base=0, channel_multiplier=1).then_inc(s_consts, 1)
            pool.wait_ge(s_consts, 1)
            pool.affine_select(out=ident[:, :], in_=ident[:, :], compare_op=ALU.not_equal, fill=1.0,
                               base=0, pattern=[[-1, P]], channel_multiplier=1)
            pool.affine_select(out=flip[:, :], in_=flip[:, :], compare_op=ALU.not_equal, fill=1.0,
                               base=1 - P, pattern=[[1, P]], channel_multiplier=1)
            pool.affine_select(out=earlier[:, :], in_=earlier[:, :], compare_op=ALU.is_ge, fill=0.0,
                               base=-1, pattern=[[1, P]], channel_multiplier=-1)
            pool.affine_select(out=same_b[:, :, :], in_=same_b[:, :, :], compare_op=ALU.is_ge, fill=0.0,
                               base=0, pattern=[[-NH, B], [0, NH]], channel_multiplier=1).then_inc(s_consts, 1)
            pool.wait_ge(s_consts, 2)
            pool.affine_select(out=same_b[:, :, :], in_=same_b[:, :, :], compare_op=ALU.is_ge, fill=0.0,
                               base=NH - 1, pattern=[[NH, B], [0, NH]], channel_multiplier=-1).then_inc(s_consts, 1)

            LOW_AT = {H + 1: (0, 1), H + 2: (6,), H + 3: (7,), H + 5: (8, 9)}

            def step(t, q4, live):
                norm, prepare, to_rows, send = live
                q = q4 % 2
                r = 1 - q

                def products(h, m):
                    pool.wait_ge(s_vcT, h + 1)
                    after(pool, s_conv, (h - 1) * LB * NC)
                    v = vcT[:, (q4 - PREPARE) % 4, 0, m, :].rearrange("p (b i) -> p i b", i=NH)
                    c = vcT[:, (q4 - PREPARE) % 4, 1, m, :].rearrange("p (b j) -> p b j", j=NH)
                    pool.tensor_tensor(kv[:, r, m],
                                       v.unsqueeze(3).to_broadcast([P, NH, B, NH]),
                                       c.unsqueeze(1).to_broadcast([P, NH, B, NH]),
                                       ALU.mult).then_inc(s_kv, 1)

                if prepare:
                    products(t - PREPARE, 0)
                if norm:
                    h = t
                    pool.wait_ge(s_ve1, h + 1)
                    pool.tensor_tensor(rstd1[:, q, :], ve1[:, q, :], neg_half[:, :], ALU.pow).then_inc(s_rstd1, 1)
                if prepare:
                    products(t - PREPARE, 1)
                if to_rows:
                    h = t - TO_ROWS
                    pool.wait_ge(s_ve2, h + 1)
                    pool.tensor_tensor(rstd2[:, r, :], ve2[:, r, :], neg_half[:, :], ALU.pow).then_inc(s_rstd2, 1)
                if send:
                    h, h4 = t - SEND, (q4 - SEND) % 4
                    routed = h + 2 - h4 % 2
                    if isinstance(h, int) and h == 0:
                        pool.wait_ge(s_setup, 9)
                    scattered(pool, h - 4, h4)
                    pool.tensor_copy(rows[:, h4, :, ID_COL],
                                     out_row[:, bass.ds(h, 1)].to_broadcast([P, TOPK])).then_inc(s_id, 1)
                    wait_apart(pool, (s_id, h + 1), (s_dest, routed), (s_wt, routed), (s_rowB, h + 1))
                    for c in range(TOPK):
                        pool.indirect_dma_start(
                            out=regions, out_offset=bass.IndirectOffsetOnAxis(ap=dest[:, h4, c:c + 1], axis=0),
                            in_=rows[:, h4, c, :], in_offset=None).then_inc(s_scat[h4], 16)
                if isinstance(t, int):
                    low_chunks(pool, LOW_AT.get(t, ()))

            steps(pool, step, [NORM, PREPARE, TO_ROWS, SEND], H, 4)
            for q in range(2):
                pool.wait_ge(s_xst[q], H // 2 * 16)

            def tile(s, q4, live):
                q = q4 % 2
                added = [] if isinstance(s, int) and s == 0 else [(s_add[1 - q], (s - 1 - (1 - q)) * 8 + 16)]
                wait_apart(pool, (s_ys, s + 1), (s_meta, s + 1), *added)
                pool.indirect_dma_start(
                    out=out_rows, out_offset=bass.IndirectOffsetOnAxis(ap=idx[q4][:, :], axis=0),
                    in_=ys[q][:, :], in_offset=None, bounds_check=TOKENS - 1, oob_is_err=False,
                    compute_op=ALU.add).then_inc(s_add[q], 16)

            steps(pool, tile, [0], TILES, 4)

        @block.scalar
        def _(act):
            def step(t, q4, live):
                norm, prepare, to_rows, gate = live
                q = q4 % 2
                r = 1 - q
                if isinstance(t, int) and t == PREPARE:
                    act.wait_ge(s_bias_ps, 1)
                    act.activation(bias_pp[:, :], mix_bank[:, 0:H], ACT.Copy).then_inc(s_bias_pp, 1)
                    act.wait_ge(s_bias_pp, 1)
                    act.wait_ge(s_consts, 3)
                if prepare:
                    h = t - PREPARE
                    act.wait_ge(s_vcps, h + 1)
                    after(act, s_z, (h - 3) * LB * NC)
                    act.activation(vcT[:, (q4 - PREPARE) % 4].rearrange("p a m t -> p (a m t)"), vc_bank[:, :], ACT.Copy).then_inc(s_vcT, 1)
                if gate:
                    h = t - ROUTE
                    act.wait_ge(s_xT2ps, h + 1)
                    after(act, s_logit, h - 1)
                    act.activation(xT2[:, q].rearrange("p m t -> p (m t)"), gate_bank[:, 0:L], ACT.Copy).then_inc(s_xT2, 1)
                    act.wait_ge(s_rowA, h + 1)
                    act.activation(rows[:, q4, 1, 0:L], rows[:, q4, 0, 0:L], ACT.Copy).then_inc(s_rowB, 1)
                if isinstance(t, int) and t == H + 3:
                    act.wait_ge(s_mixT, H * LB)
                    high_chunks(act, range(8, 9))
                if norm:
                    h = t
                    landed(act, s_x, h, q4)
                    act.activation(junk[:, :], xr[:, q4, :], ACT.Copy, accum_out=sum1[:, q, :]).then_inc(s_sum1, 1)
                    act.wait_ge(s_sum1, h + 1)
                    act.activation(nm1[:, q, :], sum1[:, q, :], ACT.Copy, scale=-1.0 / L).then_inc(s_nm1, 1)
                if gate:
                    h = t - ROUTE
                    act.wait_ge(s_logit, h + 1)
                    act.activation(th[:, q, :], gate_bank[:, L:L + E], ACT.Tanh, scale=1.0 / SOFTCAP).then_inc(s_th, 1)
                if isinstance(t, int) and t >= H:
                    if t == H:
                        act.wait_ge(s_w, 3 * E * 16)
                        act.wait_ge(s_toepps, H // 2)
                        high_chunks(act, range(0, 2))
                    if t == H + 1:
                        act.wait_ge(s_toepps, H)
                        high_chunks(act, range(2, 4))
                    if t == H + 2:
                        act.wait_ge(s_conv, H * LB * NC)
                        high_chunks(act, range(4, 8))
                if norm:
                    h = t
                    act.wait_ge(s_nm1, h + 1)
                    act.activation(junk[:, :], xr[:, q4, :], ACT.Square, bias=nm1[:, q, :],
                                   accum_out=ssq1[:, q, :]).then_inc(s_ssq1, 1)
                    act.wait_ge(s_ssq1, h + 1)
                    act.activation(ve1[:, q, :], ssq1[:, q, :], ACT.Copy, bias=LN_EPS, scale=1.0 / L).then_inc(s_ve1, 1)
                if prepare:
                    h = t - PREPARE
                    after(act, s_skps, h - 1)
                    act.activation(skip_mat[:, r, :], same_b[:, :, :].rearrange("p b j -> p (b j)"), ACT.Copy,
                                   scale=bias_pp[:, bass.ds(h, 1)]).then_inc(s_smat, 1)
                if gate and q == 1:
                    h = t - ROUTE
                    act.wait_ge(s_tmax, h + 1)
                    act.activation(nbias[:, :], tmax[:, :], ACT.Copy, scale=-SOFTCAP).then_inc(s_nb, 2)
                    act.wait_ge(s_nb, h + 1)
                    for a in range(2):
                        act.activation(ex[:, a, :], th[:, a, :], ACT.Exp, bias=nbias[:, a:a + 1], scale=SOFTCAP,
                                       accum_out=esum[:, a:a + 1]).then_inc(s_ex, 1)
                if norm:
                    h = t
                    act.wait_ge(s_rstd1, h + 1)
                    act.activation(nmr1[:, q, :], nm1[:, q, :], ACT.Copy, scale=rstd1[:, q, :]).then_inc(s_nmr1, 1)
                    act.wait_ge(s_nmr1, h + 1)
                    after(act, s_vcps, h - 1)
                    after(act, s_u, h - 1)
                    act.activation(xhat[:, q, :], xr[:, q4, :], ACT.Identity, bias=nmr1[:, q, :],
                                   scale=rstd1[:, q, :]).then_inc(s_xhat, 1)
                if to_rows:
                    h, h4 = t - TO_ROWS, (q4 - TO_ROWS) % 4
                    act.wait_ge(s_mv2, h + 1)
                    act.activation(ve2[:, r, :], mv2[:, r, 1:2], ACT.Copy, bias=LN_EPS).then_inc(s_ve2, 1)
                    act.activation(nm2[:, r, :], mv2[:, r, 0:1], ACT.Copy, scale=-1.0).then_inc(s_nm2, 1)
                if to_rows:
                    h, h4 = t - TO_ROWS, (q4 - TO_ROWS) % 4
                    act.wait_ge(s_nm2, h + 1)
                    act.wait_ge(s_rstd2, h + 1)
                    act.activation(nmr2[:, r, :], nm2[:, r, :], ACT.Copy, scale=rstd2[:, r, :]).then_inc(s_nmr2, 1)
                    act.wait_ge(s_nmr2, h + 1)
                    act.wait_ge(s_xn, h + 1)
                    scattered(act, h - 4, h4)
                    act.activation(rows[:, h4, 0, 0:L], xn[:, r, :], ACT.Identity, bias=nmr2[:, r, :],
                                   scale=rstd2[:, r, :]).then_inc(s_rowA, 1)
                if prepare:
                    h = t - PREPARE
                    act.wait_ge(s_toepps, h + 1)
                    after(act, s_conv, (h - 1) * LB * NC)
                    act.activation(toep[:, r, :], skip_bank[:, L:2 * L], ACT.Copy).then_inc(s_toep, 1)

            steps(act, step, [NORM, PREPARE, TO_ROWS, ROUTE], H, 4)
            act.activation(silu0[:, :], neg_half[:, :], ACT.Silu)
            act.wait_ge(s_base, H)
            act.wait_ge(s_mixps, H)
            act.wait_ge(s_u, H)
            high_chunks(act, range(9, CHUNKS))
            fill_behind(act, 1)

            def tile(s, q4, live):
                q = q4 % 2
                now_x, now_h, now_y = live
                if now_x:
                    act.wait_ge(s_xTps, s + 1)
                    after(act, s_h3, s - 1)
                    after(act, s_xTl, s - 1)
                    act.activation(xTh[:, q].rearrange("p m t -> p (m t)"), xT_bank[:, 0:L], ACT.Copy).then_inc(s_xT, 1)
                if now_h:
                    n, r = s - 1, 1 - q
                    act.wait_ge(s_h1, n + 1)
                    after(act, s_gated, n - 1)
                    act.activation(act1[:, r, :], h1_bank[r][:, :], ACT.Silu).then_inc(s_act, 1)
                if now_y:
                    n = s - 2
                    act.wait_ge(s_y, n + 1)
                    act.wait_ge(s_meta, n + 1)
                    if not (isinstance(n, int) and n < 2):
                        loads(act, s_add, n - 2, q)
                    act.activation(ys[q][:, :], y_bank[q][:, 0:L], ACT.Copy,
                                   scale=wt[:, (q4 - 2) % 4, :]).then_inc(s_ys, 1)

            steps(act, tile, [0, 1, 2], TILES, 4)

        @block.vector
        def _(dve):
            dve.memset(kzero[:, :], 0.0).then_inc(s_kzero, 1)
            dve.wait_ge(s_consts, 3)
            dve.tensor_copy(region[:, :], region_i[:, :]).then_inc(s_setup, 1)
            dve.tensor_copy(expert[:, :], expert_i[:, :]).then_inc(s_setup, 1)
            dve.tensor_copy(head_f[:, :], head_i[:, :]).then_inc(s_setup, 1)
            dve.tensor_copy(tile_f[:, :], tile_i[:, :]).then_inc(s_setup, 1)
            dve.tensor_copy(pid_f[:, :], pid_i[:, :]).then_inc(s_setup, 1)
            dve.tensor_scalar(pid_b[:, :], pid_i[:, :], NH.bit_length() - 1, None,
                              ALU.logical_shift_right).then_inc(s_setup, 1)
            dve.wait_ge(s_setup, 6)
            dve.tensor_copy(pid_bf[:, :], pid_b[:, :]).then_inc(s_setup, 1)
            dve.wait_ge(s_setup, 7)
            dve.scalar_tensor_tensor(row0[:, :], pid_bf[:, :], float(D - NH), pid_f[:, :], ALU.mult,
                                     ALU.add).then_inc(s_setup, 1)
            dve.wait_ge(s_setup, 8)
            dve.tensor_scalar(out_row[:, :], head_f[:, :], row0[:, :], None, ALU.add).then_inc(s_setup, 1)

            def z_bank(h, h4, m, c):
                n = (m * NC + c)
                dve.wait_ge(s_conv, h * (LB * NC) + n + 1)
                cb = vcT[:, h4, 1, m, :].rearrange("p (b i) -> p i b", i=NH)[:, c * CH:(c + 1) * CH, :]
                dve.tensor_tensor(z[:, m, c * CH:(c + 1) * CH, :].rearrange("p i (b j) -> p i b j", b=B),
                                  conv_bank[m][c][:, :].rearrange("p (i b j) -> p i b j", i=CH, b=B),
                                  cb.unsqueeze(3).to_broadcast([P, CH, B, NH]), ALU.mult).then_inc(s_z, 1)

            def sum_i(h, q, m):
                dve.wait_ge(s_z, h * (LB * NC) + (m + 1) * NC)
                after(dve, s_mixps, h - 1)
                dve.tensor_reduce(mixT[:, q, m, :], z[:, m, :, :].rearrange("p i t -> p t i"), AX.X,
                                  ALU.add).then_inc(s_mixT, 1)

            LOW_AT = {H + 2: range(2, 6)}

            def step(t, q4, live):
                prepare, convolve, to_rows, route, place = live
                q = q4 % 2
                r = 1 - q
                route = route and q == 1
                place = place and q == 0
                if to_rows:
                    z_bank(t - TO_ROWS, (q4 - TO_ROWS) % 4, 1, 1)
                if place:
                    h, a = t - PLACE, (q4 - PLACE) % 4 // 2
                    dve.wait_ge(s_mask, h + 1)
                    dve.tensor_tensor(msum_a[:, :], msum[:, a, :], mask[:, 0, :], ALU.add).then_inc(s_msum_a, 2)
                if to_rows:
                    sum_i(t - TO_ROWS, r, 1)
                if place:
                    h, a = t - PLACE, (q4 - PLACE) % 4 // 2
                    dve.wait_ge(s_msum_a, h + 1)
                    dve.tensor_tensor(msum[:, 1 - a, :], msum_a[:, :], mask[:, 1, :], ALU.add).then_inc(s_msum, 2)
                if prepare:
                    h, h4 = t - PREPARE, (q4 - PREPARE) % 4
                    dve.wait_ge(s_xhat, h + 1)
                    landed(dve, s_c, h, h4)
                    after(dve, s_skps, h - 1)
                    dve.tensor_tensor(u[:, r, :], xhat[:, r, :], cr[:, h4, :], ALU.mult).then_inc(s_u, 1)
                if convolve:
                    z_bank(t - CONVOLVE, (q4 - CONVOLVE) % 4, 0, 0)
                if route:
                    h = t - ROUTE
                    dve.wait_ge(s_th, h + 1)
                    dve.tensor_reduce(tmax[:, :], th[:, :, :], AX.X, ALU.max).then_inc(s_tmax, 2)
                if to_rows:
                    h = t - TO_ROWS
                    dve.wait_ge(s_mixps, h + 1)
                    dve.wait_ge(s_base, h + 1)
                    after(dve, s_rowA, h - 1)
                    if not (isinstance(h, int) and h < 2):
                        loads(dve, s_xst, h - 2, r)
                    dve.tensor_tensor(xn[:, r, :], mix_bank[:, 0:L], base[:, r, :], ALU.add).then_inc(s_xn, 1)
                if place:
                    h = t - PLACE
                    dve.wait_ge(s_rankps, h + 1)
                    dve.tensor_tensor(pos[:, :, :], gate_bank[:, RANKS:RANKS + 2 * E].rearrange("p (a e) -> p a e", a=2),
                                      region[:, :].unsqueeze(1).to_broadcast([P, 2, E]), ALU.add).then_inc(s_pos, 2)
                if to_rows:
                    h = t - TO_ROWS
                    dve.wait_ge(s_xn, h + 1)
                    dve.bn_stats(st2[:, r, :], xn[:, r, :]).then_inc(s_st2, 1)
                if place:
                    h = t - PLACE
                    dve.wait_ge(s_pos, h + 1)
                    dve.tensor_tensor(hpos[:, :, :, :], hot[:, :, :, :],
                                      pos[:, :, :].unsqueeze(2).to_broadcast([P, 2, TOPK, E]),
                                      ALU.mult).then_inc(s_hpos, 2)
                if place:
                    h = t - PLACE
                    dve.wait_ge(s_hpos, h + 1)
                    dve.tensor_reduce(destf[:, :, :], hpos[:, :, :, :], AX.X, ALU.add).then_inc(s_destf, 2)
                if convolve:
                    z_bank(t - CONVOLVE, (q4 - CONVOLVE) % 4, 0, 1)
                if place:
                    h, h4 = t - PLACE, (q4 - PLACE) % 4
                    dve.wait_ge(s_destf, h + 1)
                    dve.tensor_copy(dest[:, h4 - 1:h4 + 1, :], destf[:, :, :]).then_inc(s_dest, 2)
                if route:
                    h = t - ROUTE
                    dve.wait_ge(s_ex, h + 1)
                    dve.reciprocal(rsum[:, :], esum[:, :]).then_inc(s_rsum, 2)
                if to_rows:
                    h = t - TO_ROWS
                    wait_apart(dve, (s_st2, h + 1))
                    dve.bn_aggr(mv2[:, r, :], st2[:, r, :]).then_inc(s_mv2, 1)
                if route:
                    h = t - ROUTE
                    dve.wait_ge(s_rsum, h + 1)
                    dve.tensor_tensor(prob[:, :, :], ex[:, :, :], rsum[:, :].unsqueeze(2).to_broadcast([P, 2, E]),
                                      ALU.mult).then_inc(s_prob, 2)
                if convolve:
                    h, h4 = t - CONVOLVE, (q4 - CONVOLVE) % 4
                    landed(dve, s_x, h, h4)
                    dve.wait_ge(s_skps, h + 1)
                    dve.wait_ge(s_toep, h + 1)
                    dve.tensor_tensor(skip[:, :], skip_bank[:, 0:L], cr[:, h4, :], ALU.mult).then_inc(s_skip, 1)
                if route:
                    h = t - ROUTE
                    wait_apart(dve, (s_prob, h + 1))
                    for a in range(2):
                        dve.max(best[:, a, :], prob[:, a, :]).then_inc(s_best, 1)
                if convolve:
                    h, h4 = t - CONVOLVE, (q4 - CONVOLVE) % 4
                    dve.wait_ge(s_skip, h + 1)
                    dve.tensor_tensor(base[:, q, :], skip[:, :], xr[:, h4, :], ALU.add).then_inc(s_base, 1)
                if route:
                    h = t - ROUTE
                    wait_apart(dve, (s_best, h + 1))
                    for a in range(2):
                        dve.max_index(best_at[:, a, :], best[:, a, :], prob[:, a, :]).then_inc(s_best_at, 1)
                if convolve:
                    sum_i(t - CONVOLVE, q, 0)
                if route:
                    h = t - ROUTE
                    dve.wait_ge(s_best_at, h + 1)
                    dve.tensor_tensor(hot[:, :, :, :], best_at[:, :, 0:TOPK].unsqueeze(3).to_broadcast([P, 2, TOPK, E]),
                                      expert[:, :].unsqueeze(1).unsqueeze(1).to_broadcast([P, 2, TOPK, E]),
                                      ALU.is_equal).then_inc(s_hot, 2)
                    dve.tensor_copy(rows[:, q4 - 1:q4 + 1, :, W_COL], best[:, :, 0:TOPK]).then_inc(s_wt, 2)
                if convolve:
                    z_bank(t - CONVOLVE, (q4 - CONVOLVE) % 4, 1, 0)
                if route:
                    h = t - ROUTE
                    dve.wait_ge(s_hot, h + 1)
                    after(dve, s_rankps, h - 1)
                    dve.tensor_tensor(mask[:, :, :], hot[:, :, 0, :], hot[:, :, 1, :], ALU.add).then_inc(s_mask, 2)
                if isinstance(t, int):
                    low_chunks(dve, LOW_AT.get(t, ()))

            steps(dve, step, [PREPARE, CONVOLVE, TO_ROWS, ROUTE, PLACE], H, 4)

            chain = [0]

            def link(ins):
                ins.then_inc(s_tab, 1)
                chain[0] += 1
                dve.wait_ge(s_tab, chain[0])

            dve.wait_ge(s_cnt, 1)
            cnt = skip_bank[0:1, 0:E]
            link(dve.tensor_tensor(fill_at[:, :], cnt, region[0:1, :], ALU.add))
            link(dve.tensor_scalar(nt_i[:, :], cnt, float(P - 1), None, ALU.add))
            link(dve.tensor_scalar(nt_s[:, :], nt_i[:, :], P.bit_length() - 1, None, ALU.logical_shift_right))
            link(dve.tensor_copy(nt[:, :], nt_s[:, :]))
            link(dve.tensor_tensor_scan(upto[:, :], one_row[:, :], nt[:, :], 0.0, ALU.mult, ALU.add))
            link(dve.tensor_tensor(past[:, :, :], tile_f[:, :].unsqueeze(2).to_broadcast([1, TILES, E]),
                                   upto[:, :].unsqueeze(1).to_broadcast([1, TILES, E]), ALU.is_ge))
            link(dve.tensor_tensor(past_nt[:, :, :], past[:, :, :],
                                   nt[:, :].unsqueeze(1).to_broadcast([1, TILES, E]), ALU.mult))
            link(dve.tensor_reduce(eid[:, :], past[:, :, :], AX.X, ALU.add))
            link(dve.tensor_reduce(first[:, :], past_nt[:, :, :], AX.X, ALU.add))
            link(dve.tensor_scalar(tile_expert[:, :], eid[:, :], float(E - 1), None, ALU.min))
            link(dve.tensor_tensor(inside[:, :], tile_f[:, :], first[:, :], ALU.subtract))
            link(dve.tensor_scalar(reg_at[:, :], eid[:, :], float(CAP), None, ALU.mult))
            link(dve.tensor_scalar(first[:, :], inside[:, :], float(P), None, ALU.mult))
            link(dve.tensor_tensor(tile_row[:, :], first[:, :], reg_at[:, :], ALU.add))
            assert chain[0] == TABLE_STEPS
            low_chunks(dve, range(10, CHUNKS))

            def tile(s, q4, live):
                q = q4 % 2
                now_meta, now_h, now_y = live
                if now_y:
                    n = s - 2
                    dve.wait_ge(s_gTps, n + 1)
                    after(dve, s_y, n - 1)
                    dve.tensor_copy(gT[:, q].rearrange("p m t -> p (m t)"), gT_bank[:, :]).then_inc(s_gT, 1)
                if now_meta:
                    loads(dve, s_xin, s, q)
                    if not (isinstance(s, int) and s < 4):
                        loads(dve, s_add, s - 4, q)
                    dve.tensor_copy(wt[:, q4, :], xin[:, q, W_COL:W_COL + 1])
                    dve.tensor_copy(idx[q4][:, :], xin[:, q, ID_COL:ROW]).then_inc(s_meta, 1)
                if now_meta:
                    dve.wait_ge(s_xT, s + 1)
                    after(dve, s_h3, s - 1)
                    dve.tensor_tensor(xTl[:, q].rearrange("p m t -> p (m t)"), xT_bank[:, 0:L],
                                      xTh[:, q].bitcast(F32).rearrange("p m t -> p (m t)"),
                                      ALU.subtract).then_inc(s_xTl, 1)
                if now_h:
                    n, r = s - 1, 1 - q
                    dve.wait_ge(s_act, n + 1)
                    dve.wait_ge(s_h3, n + 1)
                    after(dve, s_gTps, n - 1)
                    dve.tensor_tensor(gated[:, r, :], act1[:, r, :], h3_bank[r][:, :], ALU.mult).then_inc(s_gated, 1)

            steps(dve, tile, [0, 1, 2], TILES, 4)

        @block.tensor
        def _(pe):
            pe.wait_ge(s_consts, 3)
            pe.wait_ge(s_bias, 16)
            pe.transpose(mix_bank[:, 0:H], bias_rows[:, :, :].rearrange("h b i -> h (b i)"),
                         ident[0:H, 0:H]).then_inc(s_bias_ps, 1)
            pe.wait_ge(s_wg, 16)
            pe.wait_ge(s_bias_pp, 1)

            def conv(h, q, m, c):
                after(pe, s_z, (h - 1) * (LB * NC) + m * NC + c + 1)
                for n in range(m + 1):
                    mm = pe.matmul(conv_bank[m][c][:, :],
                                   toep[:, q, (m - n) * P:(m - n + 1) * P],
                                   kv[:, q, n, c * CH:(c + 1) * CH].rearrange("p i b j -> p (i b j)"),
                                   start=(n == 0), stop=(n == m))
                mm.then_inc(s_conv, 1)

            def step(t, q4, live):
                prepare, convolve, to_rows, gate, place = live
                q = q4 % 2
                r = 1 - q
                place = place and q == 0
                if prepare:
                    h, h4 = t - PREPARE, (q4 - PREPARE) % 4
                    pe.wait_ge(s_xhat, h + 1)
                    landed(pe, s_c, h, h4)
                    after(pe, s_vcT, h)
                    for a, src in ((0, xhat[:, r, :]), (1, cr[:, h4, :])):
                        for m in range(LB):
                            mm = pe.transpose(vc_bank[:, (a * LB + m) * P:(a * LB + m + 1) * P],
                                              src[:, m * P:(m + 1) * P], ident[:, :])
                    mm.then_inc(s_vcps, 1)
                if gate:
                    h, h4 = t - ROUTE, (q4 - ROUTE) % 4
                    pe.wait_ge(s_rowA, h + 1)
                    after(pe, s_th, h)
                    after(pe, s_pos, h - 2 + q)
                    for m in range(LB):
                        mm = pe.transpose(gate_bank[:, m * P:(m + 1) * P], rows[:, h4, 0, m * P:(m + 1) * P], ident[:, :])
                    mm.then_inc(s_xT2ps, 1)
                if convolve:
                    h = t - CONVOLVE
                    pe.wait_ge(s_kv, (h + 1) * LB)
                    pe.wait_ge(s_toep, h + 1)
                    conv(h, q, 0, 0)
                if gate:
                    h = t - ROUTE
                    pe.wait_ge(s_xT2, h + 1)
                    for m in range(LB):
                        mm = pe.matmul(gate_bank[:, L:L + E], xT2[:, q, m, :], wg[:, m, :],
                                       start=(m == 0), stop=(m == LB - 1))
                    mm.then_inc(s_logit, 1)
                if convolve:
                    conv(t - CONVOLVE, q, 0, 1)
                if place:
                    h, a = t - PLACE, (q4 - PLACE) % 4 // 2
                    pe.wait_ge(s_mask, h + 1)
                    after(pe, s_msum, h - 1)
                    pe.wait_ge(s_th, h + 2 if gate else h + 1)
                    both = gate_bank[:, RANKS:RANKS + 2 * E].rearrange("p (a e) -> p a e", a=2)
                    pe.matmul(both, earlier[:, :], mask[:, :, :], start=True, stop=False)
                    pe.matmul(both, ones[:, :], msum[:, a, :].unsqueeze(1).to_broadcast([P, 2, E]), start=False, stop=False)
                    pe.matmul(gate_bank[:, RANKS + E:RANKS + 2 * E], ones16[:, :], mask[:, 0, :], start=False,
                              stop=True).then_inc(s_rankps, 2)
                if to_rows:
                    h = t - TO_ROWS
                    pe.wait_ge(s_mixT, (h + 1) * LB)
                    after(pe, s_xn, h)
                    for m in range(LB):
                        mm = pe.transpose(mix_bank[:, m * P:(m + 1) * P], mixT[:, r, m, :], ident[:, :])
                    mm.then_inc(s_mixps, 1)
                if convolve:
                    conv(t - CONVOLVE, q, 1, 0)
                    conv(t - CONVOLVE, q, 1, 1)
                if prepare:
                    h = t - PREPARE
                    pe.wait_ge(s_u, h + 1)
                    after(pe, s_skip, h)
                    pe.wait_ge(s_smat, h + 1)
                    pe.matmul(skip_bank[:, 0:L], skip_mat[:, r, :], u[:, r, :], start=True, stop=True).then_inc(s_skps, 1)
                    after(pe, s_toep, h)
                    if isinstance(h, int) and h < 4:
                        pe.wait_ge(s_diag, 16 if h == 0 else 4 * 16)
                    pe.matmul(skip_bank[:, L:2 * L], flip[:, :], hank[:, bass.ds(h, 1), :].rearrange("p a l -> p (a l)"),
                              start=True, stop=True).then_inc(s_toepps, 1)

            steps(pe, step, [PREPARE, CONVOLVE, TO_ROWS, ROUTE, PLACE], H, 4)
            pe.wait_ge(s_msum, H)
            pe.wait_ge(s_pos, H)
            pe.matmul(skip_bank[:, 0:E], ones[:, :], msum[:, H // 2 % 2, :], start=True, stop=True).then_inc(s_cnt, 1)

            pe.wait_ge(s_w, 3 * E * 16)
            pe.wait_ge(s_low, CHUNKS)
            pe.wait_ge(s_tab, TABLE_STEPS)
            pe.wait_ge(s_z, H * LB * NC)

            def products(out, r, e, which):
                for m in range(LB):
                    high = W13h[:, bass.ds(e, 1), which, m, :]
                    low = W13l[:, bass.ds(e, 1), which, m, :]
                    for x_part, w_part in ((xTh, high), (xTh, low), (xTl, high)):
                        mm = pe.matmul(out, x_part[:, r, m, :], w_part,
                                       start=(m == 0 and w_part is high and x_part is xTh),
                                       stop=(m == LB - 1 and x_part is xTl))
                return mm

            def tile(s, q4, live):
                q = q4 % 2
                now_x, now_h, now_y = live
                if now_h:
                    n, r = s - 1, 1 - q
                    e = pe.value_load(tile_expert[0:1, bass.ds(n, 1)], min_val=0, max_val=E - 1)
                    pe.wait_ge(s_xT, n + 1)
                    after(pe, s_act, n - 1)
                    pe.wait_ge(s_xTl, n + 1)
                    products(h1_bank[r][:, :], r, e, 0).then_inc(s_h1, 1)
                if now_x:
                    loads(pe, s_xin, s, q)
                    after(pe, s_xTl, s)
                    for m in range(LB):
                        mm = pe.transpose(xT_bank[:, m * P:(m + 1) * P], xin[:, q, m * P:(m + 1) * P], ident[:, :])
                    mm.then_inc(s_xTps, 1)
                if now_y:
                    n = s - 2
                    pe.wait_ge(s_gated, n + 1)
                    after(pe, s_gT, n)
                    for m in range(KB):
                        mm = pe.transpose(gT_bank[:, m * P:(m + 1) * P], gated[:, q, m * P:(m + 1) * P], ident[:, :])
                    mm.then_inc(s_gTps, 1)
                if now_h:
                    n, r = s - 1, 1 - q
                    after(pe, s_gated, n - 1)
                    products(h3_bank[r][:, :], r, e, 1).then_inc(s_h3, 1)
                if now_y:
                    n = s - 2
                    e = pe.value_load(tile_expert[0:1, bass.ds(n, 1)], min_val=0, max_val=E - 1)
                    pe.wait_ge(s_gT, n + 1)
                    after(pe, s_ys, n - 1)
                    for m in range(KB):
                        mm = pe.matmul(y_bank[q][:, 0:L], gT[:, q, m, :],
                                       W2[:, bass.ds(e, 1), m, :], start=(m == 0), stop=(m == KB - 1))
                    mm.then_inc(s_y, 1)

            steps(pe, tile, [0, 1, 2], TILES, 4)


_INS = ['x', 'fside_S2_0', 'ctx_2048', 'L0_xattn_k', 'L0_ffn_w_gate', 'L0_ffn_w1', 'L0_ffn_w3', 'L0_ffn_w2']
_OUTS = [((16, 128, 256), 'float32')]


def kernel(**inputs):
    import numpy as _np
    import concourse.bacc as _bacc
    from concourse import mybir as _mybir
    from concourse.bass_utils import run_bass_kernel_spmd as _run

    nc = _bacc.Bacc("TRN2", target_bir_lowering=False, num_devices=1)
    arrays, args = {}, []
    for name in _INS:
        a = _np.ascontiguousarray(inputs[name])
        arrays[f"in_{name}_dram"] = a
        args.append(nc.dram_tensor(f"in_{name}_dram", a.shape, _mybir.dt.from_np(a.dtype), kind="ExternalInput").ap())
    for i, (shape, dtype) in enumerate(_OUTS):
        dt = _mybir.dt.from_np(_np.dtype(dtype))
        args.append(nc.dram_tensor(f"out_{i}_dram", shape, dt, kind="ExternalOutput").ap())
    xattn_ffn_kernel(nc, *args)
    r = _run(nc, [arrays], core_ids=[0])
    got = tuple(r.results[0][f"out_{i}_dram"] for i in range(len(_OUTS)))
    return got[0]
```
